# Optimizing a Trainium2 kernel written in Bass

```python
import numpy as np
import jax
import jax.numpy as jnp

def _softmax(x, axis=-1):
    return jax.nn.softmax(x, axis=axis)

def _gelu(x):
    return jax.nn.gelu(x, approximate=True)

def _silu(x):
    return jax.nn.silu(x)

def _sigmoid(x):
    return jax.nn.sigmoid(x)

def _layernorm(x, axis=-1, eps=1e-05):
    m = jnp.mean(x, axis=axis, keepdims=True)
    v = jnp.var(x, axis=axis, keepdims=True)
    return (x - m) / jnp.sqrt(v + eps)

def _scatter_add(tgt, idx, src, axis=0):
    return tgt.at[idx].add(src)

def _segment_sum(src, seg, n):
    return jax.ops.segment_sum(src, seg, n)
kernel_name = 'mk_flamingo_gated_d1_seqx_r4_5b22e5'

def setup_inputs(seed: int=0):
    np.random.seed(seed)
    _w = jnp.asarray

    def _rec_inputs():
        import jax
        import jax.numpy as jnp
        _rk = jax.random.key(seed)
        x = -0.000125 + 0.9999 * jax.random.normal(jax.random.fold_in(_rk, 1), (4, 512, 512), jnp.float32)
        _lenS = 512 - jax.random.randint(jax.random.fold_in(_rk, 7), (4,), 0, max(1, 512 // 4) + 1, jnp.int32)
        _lenS2 = 512 - jax.random.randint(jax.random.fold_in(_rk, 8), (4,), 0, max(1, 512 // 4) + 1, jnp.int32)
        fside_BxS2xS2_0 = -3.05549e-07 + 0.0199987 * jax.random.normal(jax.random.fold_in(_rk, 11), (4, 512, 512), jnp.float32)
        _ctx_1024P = jax.random.normal(jax.random.fold_in(_rk, 12), (4, 16, 256), jnp.float32)
        _ctx_1024c = jax.random.dirichlet(jax.random.fold_in(_rk, 512), 0.3 * jnp.ones((16,), jnp.float32), (4, 512))
        _ctx_1024t = jnp.einsum('bsk,bkd->bsd', _ctx_1024c, _ctx_1024P)
        _ctx_1024t = _ctx_1024t * jax.lax.rsqrt(jnp.mean(jnp.square(_ctx_1024t)) + 1e-12) * 0.953939
        ctx_1024 = 6.82029e-06 + 0.0200006 * (_ctx_1024t + 0.3 * jax.random.normal(jax.random.fold_in(_rk, 612), (4, 512, 256), jnp.float32))
        _g = jax.random.normal(jax.random.fold_in(_rk, 9001), (2, 1), jnp.float32)
        _g = jnp.sign(_g) * jnp.maximum(jnp.abs(_g), 1.0) + (_g == 0) * 1.0
        g_xattn = _g[0]
        g_ffn = _g[1]
        return (x, fside_BxS2xS2_0, ctx_1024, g_xattn, g_ffn)
    x, fside_BxS2xS2_0, ctx_1024, g_xattn, g_ffn = _rec_inputs()

    def _L0_xattn_setup():
        import jax, jax.numpy as jnp
        import numpy as np
        EPS = 1e-06
        QMAX = 127.0

        def _smooth_quant_linear(x, w):
            amax_x = jnp.max(jnp.abs(x), axis=0)
            amax_w = jnp.max(jnp.abs(w), axis=0)
            s = jnp.sqrt(jnp.maximum(amax_x, EPS) / jnp.maximum(amax_w, EPS))
            s = jnp.maximum(s, EPS)
            xs = x / s
            ws = w * s
            x_scale = jnp.maximum(jnp.max(jnp.abs(xs), axis=-1, keepdims=True), EPS) / QMAX
            w_scale = jnp.maximum(jnp.max(jnp.abs(ws), axis=-1, keepdims=True), EPS) / QMAX
            x_q = jnp.clip(jnp.round(xs / x_scale), -QMAX, QMAX)
            w_q = jnp.clip(jnp.round(ws / w_scale), -QMAX, QMAX)
            return x_q @ w_q.T * x_scale * w_scale.T

        def _expert_forward(xe, guw, dw):
            h = _smooth_quant_linear(xe, guw)
            gate, up = jnp.split(h, 2, axis=-1)
            a = jax.nn.silu(gate) * up
            return _smooth_quant_linear(a, dw)
        key = jax.random.key(seed)
        k1, k2, k3 = jax.random.split(key, 3)
        E, T, D, I = (8, 512, 512, 256)
        x = jax.random.normal(k1, (E, T, D), dtype=jnp.float32)
        gate_up_weight = jax.random.normal(k2, (E, 2 * I, D), dtype=jnp.float32) * 0.02
        down_weight = jax.random.normal(k3, (E, D, I), dtype=jnp.float32) * 0.02
        return {'x': x, 'gate_up_weight': gate_up_weight, 'down_weight': down_weight}
    _L0_xattn_all = _L0_xattn_setup()
    _L0_xattn_in = {k: v for k, v in _L0_xattn_all.items() if k in ()}
    del _L0_xattn_all

    def _L0_ffn_setup():
        import jax, jax.numpy as jnp
        import numpy as np
        TOP_K = 2
        key = jax.random.key(seed)
        ks = jax.random.split(key, 5)
        B, T, C, E, F = (2, 512, 512, 8, 256)
        scale = 0.02
        return {'x': jax.random.normal(ks[0], (B, T, C), jnp.float32), 'w_router': jax.random.normal(ks[1], (C, E), jnp.float32) * scale, 'w1': jax.random.normal(ks[2], (E, C, F), jnp.float32) * scale, 'w3': jax.random.normal(ks[3], (E, C, F), jnp.float32) * scale, 'w2': jax.random.normal(ks[4], (E, F, C), jnp.float32) * scale}
    _L0_ffn_all = _L0_ffn_setup()
    _L0_ffn_in = {k: v for k, v in _L0_ffn_all.items() if k in ('w_router', 'w1', 'w3', 'w2')}
    del _L0_ffn_all
    return {'x': x, 'fside_BxS2xS2_0': fside_BxS2xS2_0, 'ctx_1024': ctx_1024, 'g_xattn': g_xattn, 'g_ffn': g_ffn, 'L0_ffn_w_router': _L0_ffn_in['w_router'], 'L0_ffn_w1': _L0_ffn_in['w1'], 'L0_ffn_w3': _L0_ffn_in['w3'], 'L0_ffn_w2': _L0_ffn_in['w2']}

def reference(x, fside_BxS2xS2_0, ctx_1024, g_xattn, g_ffn, L0_ffn_w_router, L0_ffn_w1, L0_ffn_w3, L0_ffn_w2):
    import jax
    import jax.numpy as jnp

    def _L0_xattn_ref(x, gate_up_weight, down_weight):
        import jax, jax.numpy as jnp
        import numpy as np
        EPS = 1e-06
        QMAX = 127.0

        def _smooth_quant_linear(x, w):
            amax_x = jnp.max(jnp.abs(x), axis=0)
            amax_w = jnp.max(jnp.abs(w), axis=0)
            s = jnp.sqrt(jnp.maximum(amax_x, EPS) / jnp.maximum(amax_w, EPS))
            s = jnp.maximum(s, EPS)
            xs = x / s
            ws = w * s
            x_scale = jnp.maximum(jnp.max(jnp.abs(xs), axis=-1, keepdims=True), EPS) / QMAX
            w_scale = jnp.maximum(jnp.max(jnp.abs(ws), axis=-1, keepdims=True), EPS) / QMAX
            x_q = jnp.clip(jnp.round(xs / x_scale), -QMAX, QMAX)
            w_q = jnp.clip(jnp.round(ws / w_scale), -QMAX, QMAX)
            return x_q @ w_q.T * x_scale * w_scale.T

        def _expert_forward(xe, guw, dw):
            h = _smooth_quant_linear(xe, guw)
            gate, up = jnp.split(h, 2, axis=-1)
            a = jax.nn.silu(gate) * up
            return _smooth_quant_linear(a, dw)
        return jax.vmap(_expert_forward)(x, gate_up_weight, down_weight)

    def _L0_ffn_ref(x, w_router, w1, w3, w2):
        import jax, jax.numpy as jnp
        import numpy as np
        TOP_K = 2
        B, T, C = x.shape
        xt = x.reshape(-1, C)
        N = xt.shape[0]
        E = w_router.shape[1]
        logits = xt @ w_router
        top_vals, top_idx = jax.lax.top_k(logits, TOP_K)
        probs = jax.nn.softmax(top_vals.astype(jnp.float32), axis=1).astype(xt.dtype)
        w = jnp.zeros((N, E), xt.dtype).at[jnp.arange(N)[:, None], top_idx].add(probs)
        g = jnp.einsum('nc,ecf->enf', xt, w1)
        u = jnp.einsum('nc,ecf->enf', xt, w3)
        h = jax.nn.silu(g) * u
        outs = jnp.einsum('enf,efc->enc', h, w2)
        y = jnp.einsum('enc,ne->nc', outs, w)
        return y.reshape(B, T, C)
    x = x + jnp.tanh(g_xattn[0]) * _L0_xattn_ref(_layernorm(x, axis=-1), fside_BxS2xS2_0, ctx_1024)
    x = x + jnp.tanh(g_ffn[0]) * _L0_ffn_ref(_layernorm(x, axis=-1), L0_ffn_w_router, L0_ffn_w1, L0_ffn_w3, L0_ffn_w2)
    return x

_drawn_inputs = setup_inputs


def setup_inputs(seed=0):
    import zlib

    import numpy as np

    out = dict(_drawn_inputs(seed))
    spreads = {}
    factors = {'L0_ffn_w_router': 2.792}
    for name, (base, spread) in spreads.items():
        noise = np.random.default_rng([zlib.crc32(name.encode()), seed]).standard_normal(out[name].shape)
        drawn = base * np.exp(spread * noise) if base else spread * noise
        out[name] = jnp.asarray(drawn.astype(out[name].dtype))
    for name, factor in factors.items():
        out[name] = (out[name] * factor).astype(out[name].dtype)
    return out
```

```python
from contextlib import ExitStack

import numpy as np

import concourse.bass as bass
from concourse import mybir

P = 128
B, T, D, F1 = 4, 512, 512, 256
E, F = 8, 256
O1 = 2 * F1
NT = T // P
CD, CF = D // P, F1 // P
NTOK = B * T
CH = NTOK // P
TILES = (2 * NTOK + E * (P - 1)) // P
AHEAD = 4
TCOLS = TILES + 2
assert (TILES - 3) % AHEAD == 0
ROW = D + 16
EPS = 1e-6
QMAX = 127.0
LN_EPS = 1e-5
MAGIC = 1.5 * 2.0 ** 23
XS, WS, HS = 2.0 ** 8, 2.0 ** 8, 2.0 ** 6

C_ID, C_TID, C_G1, C_P, C_MAG, C_NMAG, C_HALF, C_NHALF, C_EPS, C_END = 0, 128, 256, 256 + TCOLS, 298, 299, 300, 304, 308, 312
H_ID, H_TRI, H_ONE, H_PRE, H_SUM, H_IOTA, H_END = 0, 128, 256, 384, 512, 520, 648


def constant_tables():
    p = np.arange(P)
    ie = np.arange(CH * E)
    f = np.zeros((P, C_END), np.float32)
    f[:, C_ID:C_ID + P] = np.eye(P)
    f[:, C_TID:C_TID + P] = (ie // E)[None, :] * P + p[:, None]
    f[:, C_G1:C_G1 + TCOLS] = np.arange(TCOLS)[None, :] + 1
    f[:, C_P] = p
    f[:, C_MAG], f[:, C_NMAG] = MAGIC, -MAGIC
    f[:, C_HALF:C_HALF + 4], f[:, C_NHALF:C_NHALF + 4] = 0.5, -0.5
    f[:, C_EPS:C_EPS + 4] = LN_EPS
    h = np.zeros((P, H_END), np.float16)
    h[:, H_ID:H_ID + P] = np.eye(P)
    h[:, H_TRI:H_TRI + P] = p[:, None] < p[None, :]
    h[:, H_ONE:H_ONE + P] = 1.0
    same = (ie % E)[:, None] == (ie % E)[None, :]
    h[:, H_PRE:H_PRE + P] = same & ((ie // E)[:, None] < (ie // E)[None, :])
    h[:, H_SUM:H_SUM + E] = (ie % E)[:, None] == np.arange(E)[None, :]
    h[:, H_IOTA:H_IOTA + P] = p[None, :]
    return f, h


RING = 6
USES = ([("w", c) for c in range(CD)] + [("d", c) for c in range(CF)] + [("x", c) for c in range(CD)]
        + [("s", 0), ("r", 0)] + [("xq", c) for c in range(CD)] + [("wq", c) for c in range(CD)] + [("ws", 0)]
        + [("a", c) for c in range(CF)] + [("s2", 0), ("r2", 0)] + [("dq", c) for c in range(CF)] + [("ds", 0)]
        + [("aq", c) for c in range(CF)] + [("y", i) for i in range(NT)] + [("l", 0), ("l", 1)])
assert len(USES) % RING == 0
PLACE = {u: (n % RING, n // RING + 1) for n, u in enumerate(USES)}
ROUND = len(USES) // RING


def build(nc, x, guw, dww, gx, gf, wr, w1, w3, w2, cf, ch, out):
    f32, f16, bf16 = mybir.dt.float32, mybir.dt.float16, mybir.dt.bfloat16
    i32, u32 = mybir.dt.int32, mybir.dt.uint32
    ALU, ACT, AX = mybir.AluOpType, mybir.ActivationFunctionType, mybir.AxisListType
    ctx = ExitStack()
    with ctx:
        def sb(name, shape, dt=f32):
            return ctx.enter_context(nc.sbuf_tensor(name, shape, dt))

        def sem(name):
            return ctx.enter_context(nc.semaphore(name))

        x_v = x.rearrange("b (i p) d -> b p i d", p=P)
        w_v = guw.rearrange("b (i p) d -> b p i d", p=P)
        d_v = dww.rearrange("b (i p) d -> b p i d", p=P)
        out_rows = out.rearrange("b t d -> (b t) d")
        out_v = out.rearrange("b (i p) d -> b p i d", p=P)
        rows = nc.dram_tensor("rows", [NTOK, ROW], i32).ap()
        rows_v = rows.rearrange("(b i p) n -> b p i n", p=P, i=NT)
        w1_v = w1.rearrange("e (c p) f -> e p c f", p=P)
        w3_v = w3.rearrange("e (c p) f -> e p c f", p=P)
        w2_v = w2.rearrange("e (c p) d -> e p c d", p=P)

        consts = sb("consts", [P, C_END])
        consth = sb("consth", [P, H_END], f16)
        w13 = sb("w13", [P, E, CD, 2, 2 * F], f16)
        wdn = sb("wdn", [P, E, F // P, 2, D], f16)
        router = sb("router", [P, CD, E])
        logits = sb("logits", [P, CH, E])
        gate = sb("gate", [P, 2])
        cells = sb("cells", [P, 16])
        small = sb("small", [P, 160])
        arena_words = 24320
        arena = sb("arena", [P, arena_words])
        at = [0]

        def carve(shape, dt=f32):
            n = int(np.prod(shape))
            size = n if dt in (f32, i32, u32) else n // 2
            v = arena[:, at[0]:at[0] + size]
            at[0] += size
            assert at[0] <= arena_words, at[0]
            if dt is not f32:
                v = v.bitcast(dt)
            if len(shape) == 2:
                v = v.rearrange("p (a b) -> p a b", a=shape[0])
            if len(shape) == 3:
                v = v.rearrange("p (a b c) -> p a b c", a=shape[0], b=shape[1])
            return v

        x_in = [carve([NT, D]) for _ in range(2)]
        w_in = [carve([O1 // P, D]) for _ in range(2)]
        d_in = carve([D // P, F1])
        xn = carve([NT, D])
        hb = carve([NT, O1])
        ab = carve([NT, F1])
        xqT = carve([CD, T], bf16)
        wqT = carve([CD, O1], bf16)
        aqT = carve([CF, T], bf16)
        dqT = carve([CF, D], bf16)
        s_row = carve([D])
        s2_row = carve([F1])
        wsc_row = carve([O1])
        dsc_row = carve([D])
        parts_words = carve([NT, D], i32)
        parts = parts_words.rearrange("p i d -> p (i d)").bitcast(f16).rearrange("p (i h d) -> p i h d", i=NT, h=2)
        x2T = hb.rearrange("p i (c t) -> p i c t", c=CD)
        stage_w = [carve([1024]) for _ in range(3)]
        at[0] = 0
        onehot = carve([E, P], f16)
        tile_eq = carve([CH * E, TCOLS], f16)
        wtab = carve([CH, 16])
        xg = [carve([ROW], i32) for _ in range(AHEAD)]
        xT = [carve([2 * CD, P], f16) for _ in range(2)]
        sil = [carve([F]) for _ in range(2)]
        hf = [carve([F]) for _ in range(2)]
        hp = [carve([2, F], f16) for _ in range(2)]
        hT = [carve([2 * F // P, P], f16) for _ in range(2)]
        yo = [carve([D]) for _ in range(2)]
        slots = carve([TCOLS], u32)
        zero_u = carve([1], u32)
        idx_g, idx_s = carve([AHEAD], u32), carve([2], u32)
        wcols = carve([TCOLS])
        gate_cell = carve([1])
        texp = carve([TCOLS], i32)
        tcol = carve([TCOLS], i32)
        rt = [carve([CH, E]) for _ in range(14)]
        rs1 = [carve([CH]) for _ in range(8)]
        r8 = [carve([E]) for _ in range(6)]
        rT = [carve([TCOLS]) for _ in range(4)]
        rc = carve([TCOLS, E])
        tot_sb = carve([P], f16)
        mask16 = carve([CH * E], f16)

        ident = consts[:, C_ID:C_ID + P]
        ident16 = consth[:, H_ID:H_ID + P]
        mag, nmag = consts[:, C_MAG:C_MAG + 1], consts[:, C_NMAG:C_NMAG + 1]
        bns = small[:, 0:24].rearrange("p (i s) -> p i s", i=NT)
        mv = small[:, 24:32].rearrange("p (i s) -> p i s", i=NT)
        rstd = small[:, 32:36]
        wmax, dmax, xmax, amax = small[:, 36:40], small[:, 40:42], small[:, 42:46], small[:, 46:48]
        winv, dinv = small[:, 48:52], small[:, 52:54]
        sv, rv = small[:, 54:58], small[:, 58:62]
        s2v, r2v = small[:, 62:64], small[:, 64:66]
        xrm, xsc, xiv = small[:, 66:70], small[:, 70:74], small[:, 74:78]
        wrm, wsc, wiv = small[:, 78:82], small[:, 82:86], small[:, 86:90]
        arm, asc, aiv = small[:, 90:94], small[:, 94:98], small[:, 98:102]
        drm, dsc, div = small[:, 102:106], small[:, 106:110], small[:, 110:114]
        ratio, ratio2 = small[:, 114:118], small[:, 118:120]
        bns2 = small[:, 120:144].rearrange("p (i s) -> p i s", i=NT)
        mv2 = small[:, 144:152].rearrange("p (i s) -> p i s", i=NT)
        rstd2 = small[:, 152:156]

        bank = [ctx.enter_context(nc.psum_tensor(f"bank{n}", [P, 512], f32)) for n in range(8)]

        ring_full = [sem(f"ring_full{r}") for r in range(RING)]
        ring_free = [sem(f"ring_free{r}") for r in range(RING)]
        prod_full = [sem(f"prod_full{r}") for r in range(2)]
        prod_free = [sem(f"prod_free{r}") for r in range(2)]
        const_in, d_ld = sem("const_in"), sem("d_ld")
        x_ld, w_ld = [sem("x_ld0"), sem("x_ld1")], [sem("w_ld0"), sem("w_ld1")]
        stage_ld = [sem(f"stage_ld{k}") for k in range(3)]
        seeded, zeroed = sem("seeded"), sem("zeroed")
        bn_done, mv_done, rstd_done, xn_done = sem("bn_done"), sem("mv_done"), sem("rstd_done"), sem("xn_done")
        inv_done, ratio_done, sqrt_done, s_done = sem("inv_done"), sem("ratio_done"), sem("sqrt_done"), sem("s_done")
        srow_done, ws_done, wrm_done = sem("srow_done"), sem("ws_done"), sem("wrm_done")
        xs_done, xsc_done, xq_done = sem("xs_done"), sem("xsc_done"), sem("xq_done")
        wsc_done, wq_done = sem("wsc_done"), sem("wq_done")
        h_done, silu_done, a_done = sem("h_done"), sem("silu_done"), sem("a_done")
        ratio2_done, sqrt2_done, s2_done, s2row_done = sem("ratio2_done"), sem("sqrt2_done"), sem("s2_done"), sem("s2row_done")
        as_done, asc_done, aq_done = sem("as_done"), sem("asc_done"), sem("aq_done")
        ds_done, dsc_done, dq_done = sem("ds_done"), sem("dsc_done"), sem("dq_done")
        x1_done, x1_st = sem("x1_done"), [sem("x1_st0"), sem("x1_st1")]
        bn2_done, mv2_done, rstd2_done, x2_done = sem("bn2_done"), sem("mv2_done"), sem("rstd2_done"), sem("x2_done")
        hi_done, lo_done, parts_st, x2T_done = sem("hi_done"), sem("lo_done"), sem("parts_st"), sem("x2T_done")
        tanh_done, wscaled, w_hi, w_lo = sem("tanh_done"), sem("wscaled"), sem("w_hi"), sem("w_lo")
        r_step, r_exp, r_tot, r_totsb, r_pre = sem("r_step"), sem("r_exp"), sem("r_tot"), sem("r_totsb"), sem("r_pre")
        oh_ready, oh_used, eq_ready, slots_ps, slots_ready = (sem("oh_ready"), sem("oh_used"), sem("eq_ready"),
                                                              sem("slots_ps"), sem("slots_ready"))
        drm_done, r_mask, r_diff, r_wtab, r_tables = sem("drm_done"), sem("r_mask"), sem("r_diff"), sem("r_wtab"), sem("r_tables")
        yo_free = sem("yo_free")
        wtab_st, gate_open, idx_g_done, idx_s_done = sem("wtab_st"), sem("gate_open"), sem("idx_g_done"), sem("idx_s_done")
        gathered = [sem(f"gathered{q}") for q in range(AHEAD)]
        xT_ps, xT_sb, wcol_done = sem("xT_ps"), sem("xT_sb"), sem("wcol_done")
        gu_ready, sil_ready, hf_ready = sem("gu_ready"), sem("sil_ready"), sem("hf_ready")
        hhi_ready, hlo_ready, hT_ps, hT_sb = sem("hhi_ready"), sem("hlo_ready"), sem("hT_ps"), sem("hT_sb")
        y_ps, y_sb, scattered = sem("y_ps"), sem("y_sb"), sem("scattered")

        def full(eng, b, use):
            r, n = PLACE[use]
            eng.wait_ge(ring_full[r], b * ROUND + n)
            return bank[r]

        def vacant(eng, b, use):
            r, n = PLACE[use]
            eng.wait_ge(ring_free[r], b * ROUND + n)
            return bank[r]

        def taken(eng, b, use):
            r, n = PLACE[use]
            eng.wait_ge(ring_free[r], b * ROUND + n + 1)

        def made(ins, use):
            ins.then_inc(ring_full[PLACE[use][0]], 1)

        def read(ins, use):
            ins.then_inc(ring_free[PLACE[use][0]], 1)

        def batches(eng, body):
            with eng.Fori(0, B // 2) as turn:
                for par in range(2):
                    body(turn * 2 + par, par)

        def tiles(eng, body):
            body(0, 0)
            with eng.Fori(0, (TILES - 3) // AHEAD) as turn:
                for k in range(1, AHEAD + 1):
                    body(turn * AHEAD + k, k % AHEAD)
            body(TILES - 2, (TILES - 2) % AHEAD)
            body(TILES - 1, (TILES - 1) % AHEAD)

        def exists(g):
            return not isinstance(g, int) or g < TILES

        def nth(v, g):
            return v[:, g:g + 1] if isinstance(g, int) else v[:, bass.ds(g, 1)]

        def route(dve):
            n = [0]

            def step(ins):
                n[0] += 1
                ins.then_inc(r_step, 1)
                dve.wait_ge(r_step, n[0])

            def over_experts(v):
                return v.unsqueeze(2).to_broadcast([P, CH, E])

            first = consts[:, C_TID:C_TID + 1]
            lg = logits[:, :, :]
            (pref, eq, first1, l2, eq2, first2, mask, w, pad, rank, q, pb, g1, tmp) = rt
            m1, k1, m2, k2, d, p2, p1, den = rs1
            taken(dve, B - 1, ("l", 0))
            taken(dve, B - 1, ("l", 1))
            for par in range(2):
                dve.wait_ge(x1_st[par], 16 * NT * (B // 2))
            dve.wait_ge(parts_st, 1 + 16 * B)
            dve.wait_ge(w_lo, 3 * E)
            for e in range(E):
                nc.vector.memset(pref[:, :, e:e + 1], float(E - e)).then_inc(zeroed, 1)
            dve.wait_ge(zeroed, E)
            src = lg
            for m, k, eq_, hot in ((m1, k1, eq, first1), (m2, k2, eq2, first2)):
                step(nc.vector.tensor_reduce(m, src, AX.X, ALU.max))
                step(nc.vector.tensor_tensor(eq_, src, over_experts(m), ALU.is_equal))
                step(nc.vector.tensor_tensor(eq_, eq_, pref, ALU.mult))
                step(nc.vector.tensor_reduce(k, eq_, AX.X, ALU.max))
                step(nc.vector.tensor_tensor(hot, pref, over_experts(k), ALU.is_equal))
                if src is lg:
                    step(nc.vector.scalar_tensor_tensor(l2, hot, -3.0e38, lg, ALU.mult, ALU.add))
                    src = l2
            step(nc.vector.tensor_tensor(mask, first1, first2, ALU.add))
            nc.vector.tensor_copy(mask16, mask.rearrange("p a b -> p (a b)")).then_inc(r_mask, 1)
            nc.vector.tensor_tensor(d, m2, m1, ALU.subtract).then_inc(r_diff, 1)
            dve.wait_ge(r_tot, 1)
            nc.vector.tensor_copy(tot_sb, bank[0][:, 0:P]).then_inc(r_totsb, 1)
            dve.wait_ge(r_exp, 1)
            step(nc.vector.tensor_scalar(den, p2, 1.0, None, ALU.add))
            step(nc.vector.reciprocal(p1, den))
            step(nc.vector.tensor_tensor(p2, p2, p1, ALU.mult))
            step(nc.vector.tensor_tensor(w, first1, over_experts(p1), ALU.mult))
            step(nc.vector.tensor_tensor(tmp, first2, over_experts(p2), ALU.mult))
            step(nc.vector.tensor_tensor(w, w, tmp, ALU.add))
            step(nc.vector.memset(wtab, 0.0))
            nc.vector.tensor_scalar(wtab[:, :, 0:E], w, gate[:, 1:2], 1.0 / (HS * WS),
                                    ALU.mult, ALU.mult).then_inc(r_wtab, 1)
            dve.wait_ge(r_pre, 1)
            ne, te, incl, start, ones8, tmp8 = r8
            pre_ps = bank[1][:, 0:P].rearrange("p (a b) -> p a b", a=CH)
            step(nc.vector.tensor_copy(ne, bank[2][:, 0:E]))
            step(nc.vector.tensor_scalar(te, ne, 1.0 / P, (P - 1.0) / P - 127.5 / 256, ALU.mult, ALU.add))
            step(nc.vector.tensor_scalar(te, te, MAGIC, MAGIC, ALU.add, ALU.subtract))
            step(nc.vector.memset(ones8, 1.0))
            step(nc.vector.tensor_tensor_scan(incl, ones8, te, 0.0, ALU.mult, ALU.add))
            step(nc.vector.tensor_tensor(start, incl, te, ALU.subtract))

            def over_chunks(v):
                return v.unsqueeze(1).to_broadcast([P, CH, E])

            tid = consts[:, C_TID:C_TID + P].rearrange("p (a b) -> p a b", a=CH)
            step(nc.vector.tensor_tensor(pad, tid, pre_ps, ALU.subtract))
            step(nc.vector.tensor_tensor(pad, pad, over_chunks(ne), ALU.add))
            step(nc.vector.tensor_tensor(rank, pre_ps, pad, ALU.subtract))
            step(nc.vector.tensor_tensor(rank, rank, mask, ALU.mult))
            step(nc.vector.tensor_tensor(rank, rank, pad, ALU.add))
            step(nc.vector.tensor_scalar(q, rank, 1.0 / P, -127.5 / 256, ALU.mult, ALU.add))
            step(nc.vector.tensor_scalar(q, q, MAGIC, MAGIC, ALU.add, ALU.subtract))
            step(nc.vector.scalar_tensor_tensor(pb, q, -float(P), rank, ALU.mult, ALU.add))
            step(nc.vector.tensor_tensor(tmp, q, over_chunks(te), ALU.is_lt))
            step(nc.vector.tensor_tensor(g1, q, over_chunks(start), ALU.add))
            step(nc.vector.scalar_tensor_tensor(g1, g1, 1.0, tmp, ALU.add, ALU.mult))
            g1f = g1.rearrange("p a b -> p (a b)")
            per = CH * E // 4
            tiles1 = consts[:, C_G1:C_G1 + TCOLS]
            for k in range(4):
                nc.vector.tensor_tensor(tile_eq[:, k * per:(k + 1) * per, :],
                                        tiles1.unsqueeze(1).to_broadcast([P, per, TCOLS]),
                                        g1f[:, k * per:(k + 1) * per].unsqueeze(2).to_broadcast([P, per, TCOLS]),
                                        ALU.is_equal).then_inc(eq_ready, 1)
            pbf = pb.rearrange("p a b -> p (a b)")
            iota = consth[:, H_IOTA:H_IOTA + P]
            tokens = consts[:, C_TID:C_TID + P]
            with dve.Fori(0, CH) as i:
                for e in range(E):
                    dve.wait_ge(oh_used, i * E + e + 1)
                    nc.vector.tensor_scalar(onehot[:, e, :], iota, pbf[:, bass.ds(i * E + e, 1)],
                                            tokens[:, bass.ds(i * E + e, 1)],
                                            ALU.is_equal, ALU.mult).then_inc(oh_ready, 1)
            over, cnt, cl, padg = rT
            tiles1_e = tiles1.unsqueeze(2).to_broadcast([P, TCOLS, E])
            step(nc.vector.tensor_tensor(rc, tiles1_e, incl.unsqueeze(1).to_broadcast([P, TCOLS, E]), ALU.is_gt))
            step(nc.vector.tensor_reduce(cnt, rc, AX.X, ALU.add))
            step(nc.vector.tensor_scalar(cl, cnt, float(E - 1), None, ALU.min))
            step(nc.vector.tensor_copy(texp, cl))
            step(nc.vector.tensor_scalar(cnt, cnt, float(D), None, ALU.add))
            nc.vector.tensor_copy(tcol, cnt).then_inc(r_tables, 1)
            dve.wait_ge(r_tables, 1)
            step(nc.vector.tensor_scalar(over, tiles1, incl[:, E - 1:E], consts[:, C_P:C_P + 1], ALU.is_gt, ALU.mult))
            dve.wait_ge(slots_ps, 1)
            nc.vector.tensor_tensor(slots, over, bank[3][:, 0:TCOLS], ALU.add).then_inc(slots_ready, 1)

        def experts_vector(dve):
            def x_to_sbuf(g, q):
                s = q % 2
                col = dve.value_load(nth(tcol[0:1, :], g), min_val=D, max_val=D + E)
                dve.wait_ge(xT_ps, g + 1)
                nc.vector.tensor_copy(xT[s].rearrange("p a b -> p (a b)").bitcast(i32),
                                      bank[s][:, :].bitcast(i32)).then_inc(xT_sb, 1)
                nc.vector.tensor_copy(nth(wcols, g), xg[q].bitcast(f32)[:, bass.ds(col, 1)]).then_inc(wcol_done, 1)

            def h_tile(g, s):
                dve.wait_ge(sil_ready, g + 1)
                nc.vector.scalar_tensor_tensor(hf[s], bank[2 + s][:, F:2 * F], HS / (XS * WS), sil[s],
                                               ALU.mult, ALU.mult).then_inc(hf_ready, 1)
                dve.wait_ge(hhi_ready, g + 1)
                nc.vector.tensor_tensor(hp[s][:, 1, :], hf[s], hp[s][:, 0, :], ALU.subtract).then_inc(hlo_ready, 1)

            def hT_tile(g, s):
                dve.wait_ge(hT_ps, g + 1)
                nc.vector.tensor_copy(hT[s].rearrange("p a b -> p (a b)").bitcast(i32),
                                      bank[4 + s][:, 0:F].bitcast(i32)).then_inc(hT_sb, 1)

            def tile(g, q):
                hT_tile(g, q % 2)
                if exists(g + 2):
                    x_to_sbuf(g + 2, (q + 2) % AHEAD)
                if exists(g + 1):
                    h_tile(g + 1, (q + 1) % 2)

            x_to_sbuf(0, 0)
            x_to_sbuf(1, 1)
            h_tile(0, 0)
            tiles(dve, tile)

        block = ctx.enter_context(nc.Block())

        @block.sync
        def _(sp):
            sp.dma_start(consts[:, :], cf).then_inc(const_in, 16)

            def load_batch(b):
                if b >= 2:
                    sp.wait_ge(x1_st[b % 2], 16 * NT * (b // 2))
                sp.dma_start(x_in[b % 2], x_v[b]).then_inc(x_ld[b % 2], 16)
                if b >= 2:
                    full(sp, b - 2, ("wq", CD - 1))
                sp.dma_start(w_in[b % 2], w_v[b]).then_inc(w_ld[b % 2], 16)
                if b >= 1:
                    full(sp, b - 1, ("dq", CF - 1))
                sp.dma_start(d_in, d_v[b]).then_inc(d_ld, 16)

            def load_expert(e):
                for k, v in enumerate((w1_v, w3_v, w2_v)):
                    if e >= 1:
                        sp.wait_ge(w_lo, 3 * (e - 1) + k + 1)
                    a = CD if k < 2 else F // P
                    sp.dma_start(stage_w[k].rearrange("p (c f) -> p c f", c=a), v[e]).then_inc(stage_ld[k], 16)

            load_batch(0)
            sp.dma_start(consth[:, :], ch).then_inc(const_in, 16)
            sp.dma_start(gate[:, 0:1], gx.rearrange("(o a) -> o a", o=1).to_broadcast([P, 1])).then_inc(const_in, 16)
            sp.dma_start(gate[:, 1:2], gf.rearrange("(o a) -> o a", o=1).to_broadcast([P, 1])).then_inc(const_in, 16)
            sp.dma_start(router[:, :, :], wr.rearrange("(c p) e -> p c e", p=P)).then_inc(const_in, 16)
            load_expert(0)
            load_expert(1)
            for b in range(1, B):
                load_batch(b)
                load_expert(2 * b)
                load_expert(2 * b + 1)
            sp.wait_ge(r_wtab, 1)
            sp.dma_start(rows.rearrange("(c p) n -> p c n", p=P)[:, :, D:ROW],
                         wtab.rearrange("p c n -> p (c n)").bitcast(i32).rearrange("p (c n) -> p c n", c=CH)).then_inc(wtab_st, 16)

        @block.vector
        def _(dve):
            for r in range(RING):
                nc.vector.memset(cells[:, r:r + 1], 0.0).then_inc(ring_free[r], 1)
            for r in range(2):
                nc.vector.memset(cells[:, 6 + r:7 + r], 0.0).then_inc(prod_free[r], 1)
            nc.vector.memset(cells[:, 8:9], 0.0).then_inc(y_sb, 2)
            nc.vector.memset(cells[:, 9:10], 0.0).then_inc(yo_free, 1)
            nc.vector.memset(cells[:, 10:11], 0.0).then_inc(parts_st, 1)
            nc.vector.memset(cells[:, 11:12], 0.0).then_inc(oh_used, E)
            dve.wait_ge(const_in, 16 * 5)

            def absmax(b, use, dst):
                ps = full(dve, b, use)
                read(nc.vector.tensor_reduce(dst, ps[:, :], AX.X, ALU.max, apply_absolute_value=True), use)

            def row_scale(b, rm, sc, iv, rm_done, nrm, done):
                dve.wait_ge(rm_done, nrm)
                nc.vector.tensor_scalar(sc, rm, EPS, 1.0 / QMAX, ALU.max, ALU.mult).then_inc(done, 1)
                dve.wait_ge(done, b * 2 + 1)
                nc.vector.reciprocal(iv, sc).then_inc(done, 1)

            def batch(b, par):
                xi, wi = x_in[par], w_in[par]
                dve.wait_ge(x_ld[par], (b - par) * 8 + 16)
                for i in range(NT):
                    nc.vector.bn_stats(bns[:, i, :], xi[:, i, :]).then_inc(bn_done, 1)
                dve.wait_ge(bn_done, b * NT + NT)
                nc.vector.memset(cells[:, 12:13], 0.0)
                for i in range(NT):
                    nc.vector.bn_aggr(mv[:, i, :], bns[:, i, :]).then_inc(mv_done, 1)
                for c in range(CD):
                    absmax(b, ("w", c), wmax[:, c:c + 1])
                for c in range(CF):
                    absmax(b, ("d", c), dmax[:, c:c + 1])
                dve.wait_ge(rstd_done, b * 2 + 2)
                for i in range(NT):
                    nc.vector.tensor_scalar(xn[:, i, :], xi[:, i, :], mv[:, i, 0:1], rstd[:, i:i + 1],
                                            ALU.subtract, ALU.mult).then_inc(xn_done, 1)
                for c in range(CD):
                    taken(dve, b, ("w", c))
                nc.vector.tensor_scalar(winv, wmax, EPS, None, ALU.max).then_inc(inv_done, 1)
                for c in range(CF):
                    taken(dve, b, ("d", c))
                nc.vector.tensor_scalar(dinv, dmax, EPS, None, ALU.max).then_inc(inv_done, 1)
                dve.wait_ge(inv_done, b * 4 + 2)
                nc.vector.reciprocal(winv, winv).then_inc(inv_done, 1)
                nc.vector.reciprocal(dinv, dinv).then_inc(inv_done, 1)
                for c in range(CD):
                    absmax(b, ("x", c), xmax[:, c:c + 1])
                for c in range(CD):
                    taken(dve, b, ("x", c))
                dve.wait_ge(inv_done, b * 4 + 4)
                nc.vector.scalar_tensor_tensor(ratio, xmax, EPS, winv, ALU.max, ALU.mult).then_inc(ratio_done, 1)
                dve.wait_ge(sqrt_done, b + 1)
                nc.vector.tensor_scalar(sv, sv, EPS, None, ALU.max).then_inc(s_done, 1)
                dve.wait_ge(s_done, b * 2 + 1)
                nc.vector.reciprocal(rv, sv).then_inc(s_done, 1)
                ps = full(dve, b, ("r", 0))
                for i in range(NT):
                    ins = nc.vector.tensor_tensor(xn[:, i, :], xn[:, i, :], ps[:, :], ALU.mult)
                    if i < NT - 1:
                        ins.then_inc(xs_done, 1)
                    else:
                        read(ins, ("r", 0))
                dve.wait_ge(xs_done, b * NT + NT - 1)
                taken(dve, b, ("r", 0))
                nc.vector.tensor_reduce(xrm, xn[:, :, :], AX.X, ALU.max, apply_absolute_value=True).then_inc(xs_done, 1)
                row_scale(b, xrm, xsc, xiv, xs_done, b * NT + NT, xsc_done)
                dve.wait_ge(xsc_done, b * 2 + 2)
                for i in range(NT):
                    nc.vector.tensor_scalar(xn[:, i, :], xn[:, i, :], xiv[:, i:i + 1], MAGIC,
                                            ALU.mult, ALU.add).then_inc(xq_done, 1)
                for j in range(O1 // P):
                    dve.wait_ge(ws_done, b * NT + j + 1)
                    nc.vector.tensor_reduce(wrm[:, j:j + 1], wi[:, j, :], AX.X, ALU.max,
                                            apply_absolute_value=True).then_inc(wrm_done, 1)
                row_scale(b, wrm, wsc, wiv, wrm_done, b * 4 + 4, wsc_done)
                taken(dve, b, ("ws", 0))
                for i in range(NT):
                    dve.wait_ge(prod_full[i % 2], b * 4 + i // 2 + 1)
                    nc.vector.scalar_tensor_tensor(hb[:, i, :], bank[6 + i % 2][:, :], xsc[:, i:i + 1],
                                                   wsc_row, ALU.mult, ALU.mult).then_inc(prod_free[i % 2], 1)
                for i in range(NT):
                    dve.wait_ge(silu_done, b * NT + i + 1)
                    dve.wait_ge(prod_free[i % 2], b * 4 + i // 2 + 2)
                    nc.vector.tensor_tensor(ab[:, i, :], hb[:, i, 0:F1], hb[:, i, F1:O1], ALU.mult).then_inc(a_done, 1)
                for c in range(CF):
                    absmax(b, ("a", c), amax[:, c:c + 1])
                for c in range(CF):
                    taken(dve, b, ("a", c))
                nc.vector.scalar_tensor_tensor(ratio2, amax, EPS, dinv, ALU.max, ALU.mult).then_inc(ratio2_done, 1)
                dve.wait_ge(sqrt2_done, b + 1)
                nc.vector.tensor_scalar(s2v, s2v, EPS, None, ALU.max).then_inc(s2_done, 1)
                dve.wait_ge(s2_done, b * 2 + 1)
                nc.vector.reciprocal(r2v, s2v).then_inc(s2_done, 1)
                ps = full(dve, b, ("r2", 0))
                for i in range(NT):
                    ins = nc.vector.tensor_tensor(ab[:, i, :], ab[:, i, :], ps[:, 0:F1], ALU.mult)
                    if i < NT - 1:
                        ins.then_inc(as_done, 1)
                    else:
                        read(ins, ("r2", 0))
                dve.wait_ge(as_done, b * NT + NT - 1)
                taken(dve, b, ("r2", 0))
                nc.vector.tensor_reduce(arm, ab[:, :, :], AX.X, ALU.max, apply_absolute_value=True).then_inc(as_done, 1)
                row_scale(b, arm, asc, aiv, as_done, b * NT + NT, asc_done)
                dve.wait_ge(asc_done, b * 2 + 2)
                for i in range(NT):
                    nc.vector.tensor_scalar(ab[:, i, :], ab[:, i, :], aiv[:, i:i + 1], MAGIC,
                                            ALU.mult, ALU.add).then_inc(aq_done, 1)
                dve.wait_ge(ds_done, b * NT + NT)
                nc.vector.tensor_reduce(drm, d_in, AX.X, ALU.max, apply_absolute_value=True).then_inc(drm_done, 1)
                row_scale(b, drm, dsc, div, drm_done, b + 1, dsc_done)
                taken(dve, b, ("ds", 0))
                for i in range(NT):
                    dve.wait_ge(prod_full[i % 2], b * 4 + 2 + i // 2 + 1)
                    nc.vector.scalar_tensor_tensor(hb[:, i, :], bank[6 + i % 2][:, :], asc[:, i:i + 1],
                                                   dsc_row, ALU.mult, ALU.mult).then_inc(prod_free[i % 2], 1)
                dve.wait_ge(tanh_done, 1)
                for i in range(NT):
                    dve.wait_ge(prod_free[i % 2], b * 4 + 2 + i // 2 + 2)
                    nc.vector.scalar_tensor_tensor(xi[:, i, :], hb[:, i, :], gate[:, 0:1], xi[:, i, :],
                                                   ALU.mult, ALU.add).then_inc(x1_done, 1)
                for i in range(NT):
                    dve.wait_ge(x1_done, b * NT + i + 1)
                    nc.vector.bn_stats(bns2[:, i, :], xi[:, i, :]).then_inc(bn2_done, 1)
                dve.wait_ge(bn2_done, b * NT + NT)
                nc.vector.memset(cells[:, 13:14], 0.0)
                for i in range(NT):
                    nc.vector.bn_aggr(mv2[:, i, :], bns2[:, i, :]).then_inc(mv2_done, 1)
                dve.wait_ge(rstd2_done, b * 2 + 2)
                for i in range(NT):
                    nc.vector.tensor_scalar(xn[:, i, :], xi[:, i, :], mv2[:, i, 0:1], rstd2[:, i:i + 1],
                                            ALU.subtract, ALU.mult).then_inc(x2_done, 1)
                for i in range(NT):
                    dve.wait_ge(hi_done, b * NT + i + 1)
                    nc.vector.scalar_tensor_tensor(parts[:, i, 1, :], xn[:, i, :], XS, parts[:, i, 0, :],
                                                   ALU.mult, ALU.subtract).then_inc(lo_done, 1)

            batches(dve, batch)
            route(dve)
            experts_vector(dve)

        @block.scalar
        def _(act):
            act.wait_ge(const_in, 16 * 5)
            nc.scalar.activation(gate[:, :], gate[:, :], ACT.Tanh).then_inc(tanh_done, 1)

            def expert_parts(b, k):
                for k3 in range(3):
                    e = b * 2 + k
                    act.wait_ge(stage_ld[k3], e * 16 + 16)
                    st = stage_w[k3]
                    if k3 < 2:
                        dst = w13[:, bass.ds(e, 1), :, 0, k3 * F:(k3 + 1) * F].rearrange("p e c f -> p (e c) f")
                        src = st.rearrange("p (c f) -> p c f", c=CD)
                    else:
                        dst = wdn[:, bass.ds(e, 1), :, 0, :].rearrange("p e c f -> p (e c) f")
                        src = st.rearrange("p (c f) -> p c f", c=F // P)
                    nc.scalar.activation(dst, src, ACT.Copy, scale=WS).then_inc(w_hi, 1)
                    nc.scalar.activation(st, st, ACT.Copy, scale=WS).then_inc(wscaled, 1)

            def from_ring(b, use, dst, src_cols=512):
                ps = full(act, b, use)
                read(nc.scalar.activation(dst, ps[:, 0:src_cols], ACT.Copy), use)

            def quantized(b, use, dst):
                ps = full(act, b, use)
                read(nc.scalar.activation(dst, ps[:, :], ACT.Identity, bias=nmag), use)

            def batch(b, par):
                wi = w_in[par]
                expert_parts(b, 0)
                from_ring(b, ("s", 0), s_row)
                for c in range(CD):
                    quantized(b, ("xq", c), xqT[:, c, :])
                act.wait_ge(wsc_done, b * 2 + 2)
                for j in range(O1 // P):
                    nc.scalar.activation(wi[:, j, :], wi[:, j, :], ACT.Identity, bias=mag,
                                         scale=wiv[:, j:j + 1]).then_inc(wq_done, 1)
                for c in range(CD):
                    quantized(b, ("wq", c), wqT[:, c, :])
                from_ring(b, ("ws", 0), wsc_row)
                for i in range(NT):
                    act.wait_ge(prod_free[i % 2], b * 4 + i // 2 + 2)
                    nc.scalar.activation(hb[:, i, 0:F1], hb[:, i, 0:F1], ACT.Silu).then_inc(silu_done, 1)
                from_ring(b, ("s2", 0), s2_row, F1)
                act.wait_ge(dsc_done, b * 2 + 2)
                for j in range(D // P):
                    nc.scalar.activation(d_in[:, j, :], d_in[:, j, :], ACT.Identity, bias=mag,
                                         scale=div[:, j:j + 1]).then_inc(dq_done, 1)
                for c in range(CF):
                    quantized(b, ("dq", c), dqT[:, c, :])
                from_ring(b, ("ds", 0), dsc_row)
                for c in range(CF):
                    quantized(b, ("aq", c), aqT[:, c, :])
                for i in range(NT):
                    act.wait_ge(x1_done, b * NT + i + 1)
                    act.dma_start(out_v[bass.ds(b, 1), :, i, :].rearrange("a p d -> (a p) d"),
                                  x_in[par][:, i, :]).then_inc(x1_st[par], 16)
                act.wait_ge(parts_st, b * 16 + 1)
                for i in range(NT):
                    act.wait_ge(x2_done, b * NT + i + 1)
                    nc.scalar.activation(parts[:, i, 0, :], xn[:, i, :], ACT.Copy, scale=XS).then_inc(hi_done, 1)
                for i in range(NT):
                    ps = full(act, b, ("y", i))
                    read(nc.scalar.activation(x2T[:, i, :, :].rearrange("p c t -> p (c t)"), ps[:, :],
                                              ACT.Copy), ("y", i))
                for h in range(2):
                    ps = full(act, b, ("l", h))
                    read(nc.scalar.activation(logits[:, bass.ds(b * NT + 2 * h, 2), :],
                                              ps[:, 0:2 * E].rearrange("p (i e) -> p i e", i=2), ACT.Copy), ("l", h))
                act.wait_ge(lo_done, b * NT + NT)
                act.dma_start(rows_v[bass.ds(b, 1), :, :, 0:D].rearrange("a p i n -> (a p) i n"),
                              parts_words).then_inc(parts_st, 16)
                expert_parts(b, 1)

            batches(act, batch)
            act.wait_ge(r_diff, 1)
            nc.scalar.activation(rs1[5], rs1[4], ACT.Exp).then_inc(r_exp, 1)

            def silu_high(g, s):
                act.wait_ge(gu_ready, g + 1)
                nc.scalar.activation(sil[s], bank[2 + s][:, 0:F], ACT.Silu, scale=1.0 / (XS * WS)).then_inc(sil_ready, 1)
                act.wait_ge(hf_ready, g + 1)
                nc.scalar.activation(hp[s][:, 0, :], hf[s], ACT.Copy).then_inc(hhi_ready, 1)

            def tile(g, q):
                s = q % 2
                if exists(g + 1):
                    silu_high(g + 1, 1 - s)
                act.wait_ge(y_ps, g + 1)
                if not isinstance(g, int) or g >= 1:
                    act.wait_ge(yo_free, g)
                act.wait_ge(wcol_done, g + 1)
                nc.scalar.activation(yo[s], bank[6 + s][:, :], ACT.Copy, scale=nth(wcols, g)).then_inc(y_sb, 1)

            silu_high(0, 0)
            tiles(act, tile)

        @block.gpsimd
        def _(pool):
            half, nhalf = consts[:, C_HALF:C_HALF + 4], consts[:, C_NHALF:C_NHALF + 4]
            pool.wait_ge(const_in, 16 * 5)

            def inverse_root(b, var, var_done, out_, done):
                pool.wait_ge(var_done, b * NT + NT)
                nc.gpsimd.tensor_tensor(out_, var, consts[:, C_EPS:C_EPS + NT], ALU.add).then_inc(done, 1)
                pool.wait_ge(done, b * 2 + 1)
                nc.gpsimd.tensor_tensor(out_, out_, nhalf, ALU.pow).then_inc(done, 1)

            def low_parts(e):
                for k in range(3):
                    pool.wait_ge(w_hi, e * 3 + k + 1)
                    pool.wait_ge(wscaled, e * 3 + k + 1)
                    c = CD if k < 2 else F // P
                    if k < 2:
                        both = w13[:, bass.ds(e, 1), :, :, k * F:(k + 1) * F].rearrange("p e c h f -> p (e c) h f")
                    else:
                        both = wdn[:, bass.ds(e, 1), :, :, :].rearrange("p e c h f -> p (e c) h f")
                    nc.gpsimd.tensor_tensor(both[:, :, 1, :], stage_w[k].rearrange("p (c f) -> p c f", c=c),
                                            both[:, :, 0, :], ALU.subtract).then_inc(w_lo, 1)

            def batch(b, par):
                inverse_root(b, mv[:, :, 1], mv_done, rstd, rstd_done)
                pool.wait_ge(ratio_done, b + 1)
                nc.gpsimd.tensor_tensor(sv, ratio, half, ALU.pow).then_inc(sqrt_done, 1)
                taken(pool, b, ("s", 0))
                for j in range(O1 // P):
                    nc.gpsimd.tensor_tensor(w_in[par][:, j, :], w_in[par][:, j, :], s_row, ALU.mult).then_inc(ws_done, 1)
                low_parts(b * 2)
                pool.wait_ge(ratio2_done, b + 1)
                nc.gpsimd.tensor_tensor(s2v, ratio2, half[:, 0:CF], ALU.pow).then_inc(sqrt2_done, 1)
                taken(pool, b, ("s2", 0))
                for j in range(D // P):
                    nc.gpsimd.tensor_tensor(d_in[:, j, :], d_in[:, j, :], s2_row, ALU.mult).then_inc(ds_done, 1)
                inverse_root(b, mv2[:, :, 1], mv2_done, rstd2, rstd2_done)
                low_parts(b * 2 + 1)

            batches(pool, batch)

            pool.wait_ge(slots_ready, 1)
            nc.gpsimd.memset(zero_u, 0).then_inc(gate_open, 1)
            pool.wait_ge(wtab_st, 16)
            pool.wait_ge(parts_st, 1 + 16 * B)
            for par in range(2):
                pool.wait_ge(x1_st[par], 16 * NT * (B // 2))
            pool.wait_ge(gate_open, 1)

            def passed():
                return nc.gpsimd.tensor_tensor(gate_cell, consts[:, C_P:C_P + 1], consts[:, C_P:C_P + 1], ALU.mult)

            def gather(g, q):
                nc.gpsimd.tensor_copy(idx_g[:, q:q + 1], nth(slots, g)).then_inc(idx_g_done, 1)
                pool.wait_ge(idx_g_done, g + 1)
                passed()
                pool.indirect_dma_start(xg[q], None, rows, bass.IndirectOffsetOnAxis(idx_g[:, q:q + 1], 0)
                                        ).then_inc(gathered[q], 16)

            def tile(g, q):
                s = q % 2
                if exists(g + AHEAD):
                    pool.wait_ge(xT_ps, g + 1)
                    pool.wait_ge(wcol_done, g + 1)
                    gather(g + AHEAD, q)
                nc.gpsimd.tensor_copy(idx_s[:, s:s + 1], nth(slots, g)).then_inc(idx_s_done, 1)
                pool.wait_ge(idx_s_done, g + 1)
                pool.wait_ge(y_sb, g + 1 + 2)
                if isinstance(g, int) and g == 0:
                    passed()
                else:
                    pool.wait_ge(scattered, g * 16)
                    passed().then_inc(yo_free, 1)
                pool.indirect_dma_start(out_rows, bass.IndirectOffsetOnAxis(idx_s[:, s:s + 1], 0), yo[s], None,
                                        compute_op=ALU.add).then_inc(scattered, 16)

            for g in range(AHEAD):
                gather(g, g)
            tiles(pool, tile)
            for q in range(AHEAD):
                pool.wait_ge(gathered[q], 16 * ((TCOLS - 1 - q) // AHEAD + 1))
            pool.wait_ge(scattered, 16 * TILES)

        @block.tensor
        def _(pe):
            pe.wait_ge(const_in, 16 * 5)

            def spread(b, use, vec, n, at_=0):
                ps = vacant(pe, b, use)
                for c in range(n):
                    ins = nc.tensor.transpose(ps[:, c * P:(c + 1) * P], vec[:, c:c + 1].to_broadcast([P, P]), ident)
                made(ins, use)

            def turned(b, use, src, c, waits=None):
                ps = vacant(pe, b, use)
                for i in range(NT):
                    if waits:
                        waits(i)
                    ins = nc.tensor.transpose(ps[:, i * P:(i + 1) * P], src[:, i, c * P:(c + 1) * P], ident)
                made(ins, use)

            def batch(b, par):
                xi, wi = x_in[par], w_in[par]
                pe.wait_ge(w_ld[par], (b - par) * 8 + 16)
                for c in range(CD):
                    turned(b, ("w", c), wi, c)
                pe.wait_ge(d_ld, b * 16 + 16)
                for c in range(CF):
                    turned(b, ("d", c), d_in, c)
                for c in range(CD):
                    turned(b, ("x", c), xn, c, (lambda i: pe.wait_ge(xn_done, b * NT + i + 1)) if c == 0 else None)
                pe.wait_ge(s_done, b * 2 + 1)
                spread(b, ("s", 0), sv, CD)
                pe.wait_ge(s_done, b * 2 + 2)
                spread(b, ("r", 0), rv, CD)
                for c in range(CD):
                    turned(b, ("xq", c), xn, c, (lambda i: pe.wait_ge(xq_done, b * NT + i + 1)) if c == 0 else None)
                for c in range(CD):
                    turned(b, ("wq", c), wi, c, (lambda i: pe.wait_ge(wq_done, b * NT + i + 1)) if c == 0 else None)
                spread(b, ("ws", 0), wsc, O1 // P)
                for c in range(CD):
                    taken(pe, b, ("xq", c))
                    taken(pe, b, ("wq", c))
                for i in range(NT):
                    pe.wait_ge(prod_free[i % 2], b * 4 + i // 2 + 1)
                    for c in range(CD):
                        ins = nc.tensor.matmul(bank[6 + i % 2][:, :], xqT[:, c, i * P:(i + 1) * P], wqT[:, c, :],
                                               start=c == 0, stop=c == CD - 1)
                    ins.then_inc(prod_full[i % 2], 1)
                for c in range(CF):
                    turned(b, ("a", c), ab, c, (lambda i: pe.wait_ge(a_done, b * NT + i + 1)) if c == 0 else None)
                pe.wait_ge(s2_done, b * 2 + 2)
                spread(b, ("s2", 0), s2v, CF)
                spread(b, ("r2", 0), r2v, CF)
                for c in range(CF):
                    turned(b, ("dq", c), d_in, c, (lambda i: pe.wait_ge(dq_done, b * NT + i + 1)) if c == 0 else None)
                spread(b, ("ds", 0), dsc, D // P)
                for c in range(CF):
                    turned(b, ("aq", c), ab, c, (lambda i: pe.wait_ge(aq_done, b * NT + i + 1)) if c == 0 else None)
                for c in range(CF):
                    taken(pe, b, ("dq", c))
                    taken(pe, b, ("aq", c))
                for i in range(NT):
                    pe.wait_ge(prod_free[i % 2], b * 4 + 2 + i // 2 + 1)
                    for c in range(CF):
                        ins = nc.tensor.matmul(bank[6 + i % 2][:, :], aqT[:, c, i * P:(i + 1) * P], dqT[:, c, :],
                                               start=c == 0, stop=c == CF - 1)
                    ins.then_inc(prod_full[i % 2], 1)
                for i in range(NT):
                    pe.wait_ge(x2_done, b * NT + i + 1)
                    ps = vacant(pe, b, ("y", i))
                    for c in range(CD):
                        ins = nc.tensor.transpose(ps[:, c * P:(c + 1) * P], xn[:, i, c * P:(c + 1) * P], ident)
                    made(ins, ("y", i))
                for h in range(2):
                    ps = vacant(pe, b, ("l", h))
                    for i in (2 * h, 2 * h + 1):
                        taken(pe, b, ("y", i))
                        for c in range(CD):
                            ins = nc.tensor.matmul(ps[:, (i % 2) * E:(i % 2 + 1) * E], x2T[:, i, c, :], router[:, c, :],
                                                   start=c == 0, stop=c == CD - 1)
                    made(ins, ("l", h))

            batches(pe, batch)

            mask_h = mask16
            pe.wait_ge(r_mask, 1)
            nc.tensor.matmul(bank[0][:, 0:P], mask_h, consth[:, H_ONE:H_ONE + P], start=True, stop=True).then_inc(r_tot, 1)
            pe.wait_ge(r_totsb, 1)
            nc.tensor.matmul(bank[1][:, 0:P], consth[:, H_TRI:H_TRI + P], mask_h, start=True, stop=False)
            nc.tensor.matmul(bank[1][:, 0:P], tot_sb, consth[:, H_PRE:H_PRE + P], start=False, stop=True)
            nc.tensor.matmul(bank[2][:, 0:E], tot_sb, consth[:, H_SUM:H_SUM + E], start=True, stop=True).then_inc(r_pre, 1)
            pe.wait_ge(eq_ready, 4)

            def place_tokens(i, first=False, last=False):
                for e in range(E):
                    k = i * E + e
                    pe.wait_ge(oh_ready, k + 1)
                    rhs = tile_eq[:, k, :] if isinstance(k, int) else tile_eq[:, bass.ds(k, 1), :].rearrange("p k t -> p (k t)")
                    end = last and e == E - 1
                    nc.tensor.matmul(bank[3][:, 0:TCOLS], onehot[:, e, :], rhs, start=first and e == 0,
                                     stop=end).then_inc(slots_ps if end else oh_used, 1)

            place_tokens(0, first=True)
            with pe.Fori(1, CH - 1) as i:
                place_tokens(i)
            place_tokens(CH - 1, last=True)

            pe.wait_ge(r_tables, 1)

            def turn_x(g, q):
                ps = bank[q % 2][:, :].bitcast(f16)
                pe.wait_ge(gathered[q], (g - q) * (16 // AHEAD) + 16)
                for j in range(2 * CD):
                    ins = nc.tensor.transpose(ps[:, j * P:(j + 1) * P], xg[q][:, 0:D].bitcast(f16)[:, j * P:(j + 1) * P], ident16)
                ins.then_inc(xT_ps, 1)

            def three(ps, lhs, rhs, chunks):
                for c in range(chunks):
                    nc.tensor.matmul(ps, lhs(0, c), rhs(c, 0), start=c == 0, stop=False)
                    nc.tensor.matmul(ps, lhs(0, c), rhs(c, 1), start=False, stop=False)
                for c in range(chunks):
                    ins = nc.tensor.matmul(ps, lhs(1, c), rhs(c, 0), start=False, stop=c == chunks - 1)
                return ins

            def expert_of(g):
                return pe.value_load(nth(texp[0:1, :], g), min_val=0, max_val=E - 1)

            def gate_up(g, s):
                e = expert_of(g)
                pe.wait_ge(xT_sb, g + 1)
                three(bank[2 + s][:, :], lambda h, c: xT[s][:, h * CD + c, :],
                      lambda c, h: w13[:, bass.ds(e, 1), c, h, :].rearrange("p e f -> p (e f)"), CD).then_inc(gu_ready, 1)

            def turn_h(g, s):
                ps = bank[4 + s][:, 0:F].bitcast(f16)
                pe.wait_ge(hhi_ready, g + 1)
                pe.wait_ge(hlo_ready, g + 1)
                for h in range(2):
                    for c in range(F // P):
                        j = h * (F // P) + c
                        ins = nc.tensor.transpose(ps[:, j * P:(j + 1) * P], hp[s][:, h, c * P:(c + 1) * P], ident16)
                ins.then_inc(hT_ps, 1)

            def down(g, s):
                e = expert_of(g)
                pe.wait_ge(hT_sb, g + 1)
                pe.wait_ge(y_sb, g + 1)
                three(bank[6 + s][:, :], lambda h, c: hT[s][:, h * (F // P) + c, :],
                      lambda c, h: wdn[:, bass.ds(e, 1), c, h, :].rearrange("p e f -> p (e f)"), F // P).then_inc(y_ps, 1)

            def tile(g, q):
                s = q % 2
                if exists(g + 1):
                    gate_up(g + 1, 1 - s)
                turn_h(g, s)
                if exists(g + 2):
                    turn_x(g + 2, (q + 2) % AHEAD)
                down(g, s)

            turn_x(0, 0)
            turn_x(1, 1)
            gate_up(0, 0)
            tiles(pe, tile)


_INS = ["x", "fside_BxS2xS2_0", "ctx_1024", "g_xattn", "g_ffn", "L0_ffn_w_router", "L0_ffn_w1", "L0_ffn_w3", "L0_ffn_w2"]


def kernel(**inputs):
    import concourse.bacc as bacc
    from concourse.bass_utils import run_bass_kernel_spmd

    nc = bacc.Bacc("TRN2", target_bir_lowering=False, num_devices=1)
    arrays, args = {}, []
    tables = dict(zip(("table_f32", "table_f16"), constant_tables()))
    for name in _INS + list(tables):
        a = np.ascontiguousarray(tables[name] if name in tables else inputs[name])
        arrays[f"in_{name}"] = a
        args.append(nc.dram_tensor(f"in_{name}", a.shape, mybir.dt.from_np(a.dtype), kind="ExternalInput").ap())
    args.append(nc.dram_tensor("out_0", (B, T, D), mybir.dt.float32, kind="ExternalOutput").ap())
    build(nc, *args)
    r = run_bass_kernel_spmd(nc, [arrays], core_ids=[0])
    return r.results[0]["out_0"]
```

```python
from contextlib import ExitStack

import numpy as np

import concourse.bass as bass
from concourse import mybir

P = 128
B, T, D, F1 = 4, 512, 512, 256
E, F = 8, 256
O1 = 2 * F1
NT = T // P
CD, CF = D // P, F1 // P
NTOK = B * T
CH = NTOK // P
TILES = (2 * NTOK + E * (P - 1)) // P
AHEAD = 4
TCOLS = TILES + 2
assert (TILES - 3) % AHEAD == 0
EW = 16
LT = NTOK // P
ROW = D + EW
EPS = 1e-6
QMAX = 127.0
LN_EPS = 1e-5
MAGIC = 1.5 * 2.0 ** 23
XS, WS, HS = 2.0 ** 8, 2.0 ** 8, 2.0 ** 6

C_ID, C_TOK, C_REV, C_G1 = 0, P, 2 * P, 3 * P
C_MAG = C_G1 + TCOLS
C_NMAG, C_HALF, C_NHALF, C_EPS, C_E, C_IE, C_IT, C_XS, C_END = (C_MAG + 1, C_MAG + 2, C_MAG + 6, C_MAG + 10, C_MAG + 14,
                                                          C_MAG + 18, C_MAG + 26, C_MAG + 42, C_MAG + 46)
H_ID, H_TRI, H_ONE, H_PRE, H_SUM, H_IOTA, H_END = 0, 128, 256, 384, 416, 424, 552
BE = NT * E


def constant_tables():
    p = np.arange(P)
    f = np.zeros((P, C_END), np.float32)
    token = np.repeat(np.arange(CH), E)[None, :] * P + p[:, None]
    f[:, C_ID:C_ID + P] = np.eye(P)
    f[:, C_TOK:C_TOK + P] = token
    f[:, C_REV:C_REV + P] = token - (NTOK - 1)
    f[:, C_G1:C_G1 + TCOLS] = np.arange(TCOLS)[None, :] + 1
    f[:, C_MAG], f[:, C_NMAG] = MAGIC, -MAGIC
    f[:, C_HALF:C_HALF + 4], f[:, C_NHALF:C_NHALF + 4] = 0.5, -0.5
    f[:, C_EPS:C_EPS + 4] = LN_EPS
    f[:, C_E:C_E + 4] = np.e
    f[:, C_IE:C_IE + E] = np.arange(E)
    f[:, C_IT:C_IT + LT] = np.arange(LT)
    f[:, C_XS:C_XS + 4] = XS
    h = np.zeros((P, H_END), np.float16)
    h[:, H_ID:H_ID + P] = np.eye(P)
    h[:, H_TRI:H_TRI + P] = p[:, None] < p[None, :]
    h[:, H_ONE:H_ONE + P] = 1.0
    ie = np.arange(BE)
    same = (ie % E)[:, None] == (ie % E)[None, :]
    h[:BE, H_PRE:H_PRE + BE] = same & ((ie // E)[:, None] < (ie // E)[None, :])
    h[:BE, H_SUM:H_SUM + E] = (ie % E)[:, None] == np.arange(E)[None, :]
    h[:, H_IOTA:H_IOTA + P] = p[None, :]
    return f, h


RING = 4
FRONT = ([("w", c) for c in range(CD)] + [("x", c) for c in range(CD)] + [("s", 0), ("r", 0)]
         + [("xq", c) for c in range(CD)] + [("wq", c) for c in range(CD)] + [("ws", 0)] + [("h", i) for i in range(NT)])
BACK = ([("d", c) for c in range(CF)] + [("a", c) for c in range(CF)] + [("s2", 0), ("r2", 0)]
        + [("aq", c) for c in range(CF)] + [("dq", c) for c in range(CF)] + [("ds", 0)] + [("o", i) for i in range(NT)]
        + [("y", i) for i in range(NT)] + [("l", 0), ("tot", 0), ("pre", 0), ("slot", 0)])
PLACE = {}
for base, uses in ((0, FRONT), (RING, BACK)):
    for n, u in enumerate(uses):
        PLACE[u] = (base + n % RING, n // RING + 1, len(range(n % RING, len(uses), RING)))


def build(nc, x, guw, dww, gx, gf, wr, w1, w3, w2, cf, ch, out):
    f32, f16, bf16 = mybir.dt.float32, mybir.dt.float16, mybir.dt.bfloat16
    i32, u32 = mybir.dt.int32, mybir.dt.uint32
    ALU, ACT, AX = mybir.AluOpType, mybir.ActivationFunctionType, mybir.AxisListType
    ctx = ExitStack()
    with ctx:
        def sb(name, shape, dt=f32):
            return ctx.enter_context(nc.sbuf_tensor(name, shape, dt))

        def sem(name):
            return ctx.enter_context(nc.semaphore(name))

        x_v = x.rearrange("b (i p) d -> b p i d", p=P)
        w_v = guw.rearrange("b (i p) d -> b p i d", p=P)
        d_v = dww.rearrange("b (i p) d -> b p i d", p=P)
        out_rows = out.rearrange("b t d -> (b t) d")
        out_v = out.rearrange("b (i p) d -> b p i d", p=P)
        rows = nc.dram_tensor("rows", [NTOK, ROW], i32).ap()
        rows_v = rows.rearrange("(b i p) n -> b p i n", p=P, i=NT)
        w1_v = w1.rearrange("e (c p) f -> e p c f", p=P)
        w3_v = w3.rearrange("e (c p) f -> e p c f", p=P)
        w2_v = w2.rearrange("e (c p) d -> e p c d", p=P)

        consts = sb("consts", [P, C_END])
        consth = sb("consth", [P, H_END], f16)
        w13 = sb("w13", [P, E, CD, 2, 2 * F], f16)
        wdn = sb("wdn", [P, E, F // P, 2, D], f16)
        router = sb("router", [P, CD, E])
        gate = sb("gate", [P, 2])
        gate_cell = sb("gate_cell", [P, 4])
        cells = sb("cells", [P, 32])
        small = sb("small", [P, 168])
        slot_sum = sb("slot_sum", [P, E, LT])
        taken_n = sb("taken_n", [P, E])
        arena_words = 26100
        arena = sb("arena", [P, arena_words])
        at = [0]

        def carve(shape, dt=f32):
            n = int(np.prod(shape))
            size = n if dt in (f32, i32, u32) else n // 2
            v = arena[:, at[0]:at[0] + size]
            at[0] += size
            assert at[0] <= arena_words, at[0]
            if dt is not f32:
                v = v.bitcast(dt)
            if len(shape) == 2:
                v = v.rearrange("p (a b) -> p a b", a=shape[0])
            if len(shape) == 3:
                v = v.rearrange("p (a b c) -> p a b c", a=shape[0], b=shape[1])
            return v

        x_in = carve([NT, D])
        w_in = carve([O1 // P, D])
        xn = carve([NT, D])
        hb = carve([NT, O1])
        xqT = carve([CD, T], bf16)
        wqT = carve([CD, O1], bf16)
        s_row, wsc_row = carve([D]), carve([O1])
        ab = carve([NT, F1])
        d_in = carve([D // P, F1])
        aqT = carve([CF, T], bf16)
        dqT = carve([CF, D], bf16)
        s2_row, dsc_row = carve([F1]), carve([D])
        x_res = carve([NT, D])
        x2 = carve([NT, D])
        x2T = carve([2, CD, P])
        row_words = carve([NT, ROW], i32)
        ohot = carve([2, NT, P], f16)
        stage_w = [carve([1024]) for _ in range(3)]

        def part(h):
            return row_words[:, :, h * (D // 2):(h + 1) * (D // 2)].bitcast(f16)

        wrow = row_words[:, :, D:ROW].bitcast(f32)
        at[0] = 0
        xg = [carve([ROW], i32) for _ in range(AHEAD)]
        xT = [carve([2 * CD, P], f16) for _ in range(2)]
        sil = [carve([F]) for _ in range(2)]
        hf = [carve([F]) for _ in range(2)]
        hp = [carve([2, F], f16) for _ in range(2)]
        hT = [carve([2 * F // P, P], f16) for _ in range(2)]
        yo = [carve([D]) for _ in range(2)]
        slots = carve([E * LT], u32)
        idx_g, idx_s = carve([AHEAD], u32), carve([2], u32)
        wcols = carve([TCOLS])
        t_expert, t_wcol, t_list = carve([TCOLS], i32), carve([TCOLS], i32), carve([TCOLS], i32)
        te, incl, ones8 = carve([E]), carve([E]), carve([E])
        ended, ended_te = carve([TCOLS, E]), carve([TCOLS, E])
        cnt, lim, fst, tmp_t = carve([TCOLS]), carve([TCOLS]), carve([TCOLS]), carve([TCOLS])

        ident = consts[:, C_ID:C_ID + P]
        ident16 = consth[:, H_ID:H_ID + P]
        mag, nmag = consts[:, C_MAG:C_MAG + 1], consts[:, C_NMAG:C_NMAG + 1]
        used = [0]

        def vec(n):
            used[0] += n
            return small[:, used[0] - n:used[0]]

        bns = vec(24).rearrange("p (i s) -> p i s", i=NT)
        mv = vec(8).rearrange("p (i s) -> p i s", i=NT)
        rstd, wmax, xmax, winv, ratio = vec(NT), vec(CD), vec(CD), vec(CD), vec(CD)
        sv, rv = vec(CD), vec(CD)
        xrm, xsc, xiv = vec(NT), vec(NT), vec(NT)
        wrm, wsc, wiv = vec(4), vec(4), vec(4)
        dmax, amax, dinv, ratio2, s2v, r2v = vec(CF), vec(CF), vec(CF), vec(CF), vec(CF), vec(CF)
        arm, asc, aiv = vec(NT), vec(NT), vec(NT)
        drm, dsc, div = vec(4), vec(4), vec(4)
        bns2 = vec(24).rearrange("p (i s) -> p i s", i=NT)
        mv2 = vec(8).rearrange("p (i s) -> p i s", i=NT)
        rstd2 = vec(NT)
        route_f = sb("route_f", [P, 11, NT, E])
        lg, mx, idf, first1, first2, mask, idle, rank, q, pb, tmp = (route_f[:, k] for k in range(11))
        mi = sb("mi", [P, NT, E], u32)
        diff, ex, den, p1, p2 = (sb(n, [P, NT]) for n in ("diff", "ex", "den", "p1", "p2"))
        mask16 = sb("mask16", [P, BE], f16)
        tot16 = sb("tot16", [BE, P], f16)
        tile_is = sb("tile_is", [P, NT, E, LT], f16)

        bank = [ctx.enter_context(nc.psum_tensor(f"bank{n}", [P, 512], f32)) for n in range(8)]

        ring_full = [sem(f"ring_full{r}") for r in range(2 * RING)]
        ring_free = [sem(f"ring_free{r}") for r in range(2 * RING)]
        const_in, x_ld, w_ld, d_ld, xr_ld = sem("const_in"), sem("x_ld"), sem("w_ld"), sem("d_ld"), sem("xr_ld")
        stage_ld = [sem(f"stage_ld{k}") for k in range(3)]
        bn_done, mv_done, rstd_done, xn_done = sem("bn_done"), sem("mv_done"), sem("rstd_done"), sem("xn_done")
        winv_done, ratio_done, sqrt_done, s_done = sem("winv_done"), sem("ratio_done"), sem("sqrt_done"), sem("s_done")
        ws_done, wrm_done, wsc_done, wq_done = sem("ws_done"), sem("wrm_done"), sem("wsc_done"), sem("wq_done")
        xs_done, xsc_done, xq_done = sem("xs_done"), sem("xsc_done"), sem("xq_done")
        silu_done, a_done = sem("silu_done"), sem("a_done")
        dinv_done, ratio2_done, sqrt2_done, s2_done = sem("dinv_done"), sem("ratio2_done"), sem("sqrt2_done"), sem("s2_done")
        as_done, asc_done, aq_done = sem("as_done"), sem("asc_done"), sem("aq_done")
        ds_done, drm_done, dsc_done, dq_done = sem("ds_done"), sem("drm_done"), sem("dsc_done"), sem("dq_done")
        x1_done, x1_st = sem("x1_done"), sem("x1_st")
        bn2_done, mv2_done, rstd2_done, x2_done = sem("bn2_done"), sem("mv2_done"), sem("rstd2_done"), sem("x2_done")
        hi_done, lo_done, rows_st = sem("hi_done"), sem("lo_done"), sem("rows_st")
        tanh_done, wscaled, w_hi, w_lo = sem("tanh_done"), sem("wscaled"), sem("w_hi"), sem("w_lo")
        r_step, r_mask, r_diff, r_exp, r_w = sem("r_step"), sem("r_mask"), sem("r_diff"), sem("r_exp"), sem("r_w")
        oh_ready, oh_used = sem("oh_ready"), sem("oh_used")
        r_tables, r_slots = sem("r_tables"), sem("r_slots")
        yo_free = sem("yo_free")
        idx_g_done, idx_s_done = sem("idx_g_done"), sem("idx_s_done")
        gathered = [sem(f"gathered{q_}") for q_ in range(AHEAD)]
        xT_ps, xT_sb, wcol_done = sem("xT_ps"), sem("xT_sb"), sem("wcol_done")
        gu_ready, sil_ready, hf_ready = sem("gu_ready"), sem("sil_ready"), sem("hf_ready")
        hhi_ready, hlo_ready, hT_ps, hT_sb = sem("hhi_ready"), sem("hlo_ready"), sem("hT_ps"), sem("hT_sb")
        y_ps, y_sb, scattered = sem("y_ps"), sem("y_sb"), sem("scattered")

        def full(eng, b, use):
            r, n, per = PLACE[use]
            eng.wait_ge(ring_full[r], b * per + n)
            return bank[r]

        def vacant(eng, b, use):
            r, n, per = PLACE[use]
            eng.wait_ge(ring_free[r], b * per + n)
            return bank[r]

        def taken(eng, b, use):
            r, n, per = PLACE[use]
            eng.wait_ge(ring_free[r], b * per + n + 1)

        def made(ins, use):
            ins.then_inc(ring_full[PLACE[use][0]], 1)

        def read(ins, use):
            ins.then_inc(ring_free[PLACE[use][0]], 1)

        def rows_of_batches(eng, step):
            step(0, None)
            with eng.Fori(1, B) as b:
                step(b, b - 1)
            step(None, B - 1)

        def tiles(eng, body):
            body(0, 0)
            with eng.Fori(0, (TILES - 3) // AHEAD) as turn:
                for k in range(1, AHEAD + 1):
                    body(turn * AHEAD + k, k % AHEAD)
            body(TILES - 2, (TILES - 2) % AHEAD)
            body(TILES - 1, (TILES - 1) % AHEAD)

        def exists(g):
            return not isinstance(g, int) or g < TILES

        def nth(v, g):
            return v[:, g:g + 1] if isinstance(g, int) else v[:, bass.ds(g, 1)]

        def row_of(v, b):
            return v[b] if isinstance(b, int) else v[bass.ds(b, 1)].rearrange("a p i n -> (a p) i n")

        o_tmp = ab.rearrange("p i f -> p (i f)").rearrange("p (k d) -> p k d", k=2)
        zeroed, rt_done, r_place, t_step = sem("zeroed"), sem("rt_done"), sem("r_place"), sem("t_step")
        xs_const = consts[:, C_XS:C_XS + NT]
        PLACES = 13

        block = ctx.enter_context(nc.Block())

        @block.sync
        def _(sp):
            sp.dma_start(x_in, x_v[0]).then_inc(x_ld, 16)
            sp.dma_start(consts[:, :], cf).then_inc(const_in, 16)
            sp.dma_start(w_in, w_v[0]).then_inc(w_ld, 16)
            sp.dma_start(consth[:, :], ch).then_inc(const_in, 16)
            sp.dma_start(gate[:, 0:1], gx.rearrange("(o a) -> o a", o=1).to_broadcast([P, 1])).then_inc(const_in, 16)
            sp.dma_start(gate[:, 1:2], gf.rearrange("(o a) -> o a", o=1).to_broadcast([P, 1])).then_inc(const_in, 16)
            sp.dma_start(router[:, :, :], wr.rearrange("(c p) e -> p c e", p=P)).then_inc(const_in, 16)

            def load_expert(e):
                for k, v in enumerate((w1_v, w3_v, w2_v)):
                    if e >= 1:
                        sp.wait_ge(w_lo, e * 3)
                    a = CD if k < 2 else F // P
                    sp.dma_start(stage_w[k].rearrange("p (c f) -> p c f", c=a), v[e]).then_inc(stage_ld[k], 16)

            for b in range(B):
                if b == 0:
                    load_expert(0)
                if b + 1 < B:
                    sp.wait_ge(xn_done, NT * (b + 1))
                    sp.dma_start(x_in, x_v[b + 1]).then_inc(x_ld, 16)
                if b >= 1:
                    full(sp, b - 1, ("dq", CF - 1))
                sp.dma_start(d_in, d_v[b]).then_inc(d_ld, 16)
                if b + 1 < B:
                    full(sp, b, ("wq", CD - 1))
                    sp.dma_start(w_in, w_v[b + 1]).then_inc(w_ld, 16)
                load_expert(b * 2 + 1)
                if b >= 1:
                    sp.wait_ge(x1_st, 16 * b)
                    sp.wait_ge(x2_done, NT * b)
                sp.dma_start(x_res, x_v[b]).then_inc(xr_ld, 16)
                if b + 1 < B:
                    load_expert(b * 2 + 2)

        @block.vector
        def _(dve):
            def absmax(b, use, dst):
                ps = full(dve, b, use)
                read(nc.vector.tensor_reduce(dst, ps[:, :], AX.X, ALU.max, apply_absolute_value=True), use)

            def row_scale(b, rm, sc, iv, rm_done, nrm, done):
                dve.wait_ge(rm_done, nrm)
                nc.vector.tensor_scalar(sc, rm, EPS, 1.0 / QMAX, ALU.max, ALU.mult).then_inc(done, 1)
                dve.wait_ge(done, b * 2 + 1)
                nc.vector.reciprocal(iv, sc).then_inc(done, 1)

            def inverse_max(b, m, inv, done, last_use):
                for u in last_use:
                    taken(dve, b, u)
                nc.vector.tensor_scalar(inv, m, EPS, None, ALU.max).then_inc(done, 1)
                dve.wait_ge(done, b * 2 + 1)
                nc.vector.reciprocal(inv, inv).then_inc(done, 1)

            def s_and_inverse(b, v, inv, root_done, done):
                dve.wait_ge(root_done, b + 1)
                nc.vector.tensor_scalar(v, v, EPS, None, ALU.max).then_inc(done, 1)
                dve.wait_ge(done, b * 2 + 1)
                nc.vector.reciprocal(inv, v).then_inc(done, 1)

            def statistics(b, src, st, ag, st_done, ag_done, cell, per_tile=None):
                for i in range(NT):
                    if per_tile is not None:
                        dve.wait_ge(per_tile, b * NT + i + 1)
                        nc.vector.memset(cells[:, cell + 1 + i:cell + 2 + i], 0.0)
                    nc.vector.bn_stats(st[:, i, :], src[:, i, :]).then_inc(st_done, 1)
                dve.wait_ge(st_done, b * NT + NT)
                nc.vector.memset(cells[:, cell:cell + 1], 0.0)
                for i in range(NT):
                    nc.vector.bn_aggr(ag[:, i, :], st[:, i, :]).then_inc(ag_done, 1)

            def scale_quantize(b, buf, width, use, rm, sc, iv, done, sc_done, q_done):
                ps = full(dve, b, use)
                for i in range(NT):
                    ins = nc.vector.tensor_tensor(buf[:, i, :], buf[:, i, :], ps[:, 0:width], ALU.mult)
                    if i < NT - 1:
                        ins.then_inc(done, 1)
                    else:
                        read(ins, use)
                dve.wait_ge(done, b * NT + NT - 1)
                taken(dve, b, use)
                nc.vector.tensor_reduce(rm, buf, AX.X, ALU.max, apply_absolute_value=True).then_inc(done, 1)
                row_scale(b, rm, sc, iv, done, b * NT + NT, sc_done)
                dve.wait_ge(sc_done, b * 2 + 2)
                for i in range(NT):
                    nc.vector.tensor_scalar(buf[:, i, :], buf[:, i, :], iv[:, i:i + 1], MAGIC,
                                            ALU.mult, ALU.add).then_inc(q_done, 1)

            def f_stats(b):
                dve.wait_ge(x_ld, b * 16 + 16)
                statistics(b, x_in, bns, mv, bn_done, mv_done, 0)

            def f_wmax(b):
                for c in range(CD):
                    absmax(b, ("w", c), wmax[:, c:c + 1])
                inverse_max(b, wmax, winv, winv_done, [("w", c) for c in range(CD)])

            def f_norm(b):
                dve.wait_ge(rstd_done, b * 2 + 2)
                for i in range(NT):
                    nc.vector.tensor_scalar(xn[:, i, :], x_in[:, i, :], mv[:, i, 0:1], rstd[:, i:i + 1],
                                            ALU.subtract, ALU.mult).then_inc(xn_done, 1)

            def f_xmax(b):
                for c in range(CD):
                    absmax(b, ("x", c), xmax[:, c:c + 1])
                for c in range(CD):
                    taken(dve, b, ("x", c))
                dve.wait_ge(winv_done, b * 2 + 2)
                nc.vector.scalar_tensor_tensor(ratio, xmax, EPS, winv, ALU.max, ALU.mult).then_inc(ratio_done, 1)

            def f_s(b):
                s_and_inverse(b, sv, rv, sqrt_done, s_done)

            def f_quant(b):
                scale_quantize(b, xn, D, ("r", 0), xrm, xsc, xiv, xs_done, xsc_done, xq_done)

            def f_wscale(b):
                for j in range(O1 // P):
                    dve.wait_ge(ws_done, b * 4 + j + 1)
                    nc.vector.tensor_reduce(wrm[:, j:j + 1], w_in[:, j, :], AX.X, ALU.max,
                                            apply_absolute_value=True).then_inc(wrm_done, 1)
                row_scale(b, wrm, wsc, wiv, wrm_done, b * 4 + 4, wsc_done)

            def f_h(b):
                taken(dve, b, ("ws", 0))
                for i in range(NT):
                    ps = full(dve, b, ("h", i))
                    read(nc.vector.scalar_tensor_tensor(hb[:, i, :], ps[:, :], xsc[:, i:i + 1], wsc_row,
                                                        ALU.mult, ALU.mult), ("h", i))

            def f_a(b):
                for i in range(NT):
                    dve.wait_ge(silu_done, b * NT + i + 1)
                    taken(dve, b, ("h", i))
                    nc.vector.tensor_tensor(ab[:, i, :], hb[:, i, 0:F1], hb[:, i, F1:O1], ALU.mult).then_inc(a_done, 1)

            def b_max(b):
                for c in range(CF):
                    absmax(b, ("d", c), dmax[:, c:c + 1])
                inverse_max(b, dmax, dinv, dinv_done, [("d", c) for c in range(CF)])
                for c in range(CF):
                    absmax(b, ("a", c), amax[:, c:c + 1])
                for c in range(CF):
                    taken(dve, b, ("a", c))
                dve.wait_ge(dinv_done, b * 2 + 2)
                nc.vector.scalar_tensor_tensor(ratio2, amax, EPS, dinv, ALU.max, ALU.mult).then_inc(ratio2_done, 1)

            def b_s(b):
                s_and_inverse(b, s2v, r2v, sqrt2_done, s2_done)

            def b_quant(b):
                scale_quantize(b, ab, F1, ("r2", 0), arm, asc, aiv, as_done, asc_done, aq_done)

            def b_dscale(b):
                dve.wait_ge(ds_done, b * 4 + 4)
                nc.vector.tensor_reduce(drm, d_in, AX.X, ALU.max, apply_absolute_value=True).then_inc(drm_done, 1)
                row_scale(b, drm, dsc, div, drm_done, b + 1, dsc_done)

            def b_out(b):
                taken(dve, b, ("ds", 0))
                for i in range(NT):
                    if i >= 2:
                        dve.wait_ge(x1_done, b * NT + i - 1)
                    ps = full(dve, b, ("o", i))
                    read(nc.vector.scalar_tensor_tensor(o_tmp[:, i % 2, :], ps[:, :], asc[:, i:i + 1], dsc_row,
                                                        ALU.mult, ALU.mult), ("o", i))

            def b_stats(b):
                statistics(b, x_res, bns2, mv2, bn2_done, mv2_done, 5, per_tile=x1_done)

            def b_norm(b):
                dve.wait_ge(rstd2_done, b * 3 + 3)
                for i in range(NT):
                    nc.vector.tensor_scalar(x2[:, i, :], x_res[:, i, :], mv2[:, i, 0:1], rstd2[:, i:i + 1],
                                            ALU.subtract, ALU.mult).then_inc(x2_done, 1)

            counted = [0]

            def over_experts(v):
                return v.unsqueeze(2).to_broadcast([P, NT, E])

            def over_tiles(v):
                return v.unsqueeze(1).to_broadcast([P, NT, E])

            def flat(v):
                return v.rearrange("p a b -> p (a b)")

            def columns(lo, b):
                v = consts[:, lo:lo + P].rearrange("p (b n) -> p b n", b=B)
                v = v[:, b, :] if isinstance(b, int) else v[:, bass.ds(b, 1), :].rearrange("p b n -> p (b n)")
                return v.rearrange("p (i e) -> p i e", i=NT)

            STEPS = 13

            def b_top(b):
                n = [0]

                def step(ins):
                    n[0] += 1
                    ins.then_inc(r_step, 1)

                def after():
                    dve.wait_ge(r_step, b * STEPS + n[0])

                taken(dve, b, ("l", 0))
                nc.vector.memset(cells[:, 10:11], 0.0)
                for i in range(NT):
                    step(nc.vector.max(mx[:, i, :], lg[:, i, :]))
                after()
                nc.vector.memset(cells[:, 11:12], 0.0)
                for i in range(NT):
                    step(nc.vector.max_index(mi[:, i, :], mx[:, i, :], lg[:, i, :]))
                nc.vector.tensor_tensor(diff[:, :], mx[:, :, 1], mx[:, :, 0], ALU.subtract).then_inc(r_diff, 1)
                after()
                step(nc.vector.tensor_copy(idf, mi[:, :, :]))
                after()
                experts = over_tiles(consts[:, C_IE:C_IE + E])
                step(nc.vector.tensor_tensor(first1, experts, over_experts(idf[:, :, 0]), ALU.is_equal))
                step(nc.vector.tensor_tensor(first2, experts, over_experts(idf[:, :, 1]), ALU.is_equal))
                after()
                nc.vector.tensor_tensor(mask16[:, :].rearrange("p (a b) -> p a b", a=NT), first1, first2,
                                        ALU.add).then_inc(r_mask, 1)
                step(nc.vector.tensor_tensor(mask, first1, first2, ALU.add))
                after()
                step(nc.vector.scalar_tensor_tensor(idle, mask, 1.0, columns(C_REV, b), ALU.subtract, ALU.mult))
                assert n[0] == STEPS

            def b_place(b):
                n = [0]

                def step(ins):
                    n[0] += 1
                    ins.then_inc(r_place, 1)

                def after():
                    dve.wait_ge(r_place, b * PLACES + n[0])

                dve.wait_ge(r_step, b * STEPS + STEPS)
                dve.wait_ge(r_exp, b + 1)
                step(nc.vector.tensor_scalar(den[:, :], ex[:, :], 1.0, None, ALU.add))
                after()
                step(nc.vector.reciprocal(p1[:, :], den[:, :]))
                ps = full(dve, b, ("tot", 0))
                read(nc.vector.tensor_copy(tot16[:, :], ps[0:BE, 0:P]), ("tot", 0))
                after()
                step(nc.vector.tensor_tensor(p2[:, :], ex[:, :], p1[:, :], ALU.mult))
                step(nc.vector.tensor_tensor(tmp, first1, over_experts(p1[:, :]), ALU.mult))
                after()
                step(nc.vector.tensor_tensor(pb, first2, over_experts(p2[:, :]), ALU.mult))
                after()
                step(nc.vector.tensor_tensor(tmp, tmp, pb, ALU.add))
                dve.wait_ge(rows_st, b * 16 + 1)
                after()
                nc.vector.tensor_scalar(wrow[:, :, 0:E], tmp, gate[:, 1:2], 1.0 / (HS * WS),
                                        ALU.mult, ALU.mult).then_inc(r_w, 1)
                ps = full(dve, b, ("pre", 0))
                step(nc.vector.tensor_tensor(rank, ps[:, 0:BE].rearrange("p (a b) -> p a b", a=NT), idle, ALU.add))
                after()
                step(nc.vector.tensor_tensor(rank, rank, over_tiles(taken_n[:, :]), ALU.add))
                after()
                read(nc.vector.tensor_tensor(taken_n[:, :], ps[:, BE:BE + E], taken_n[:, :], ALU.add), ("pre", 0))
                step(nc.vector.tensor_scalar(q, rank, 1.0 / P, -127.5 / 256, ALU.mult, ALU.add))
                after()
                step(nc.vector.tensor_scalar(q, q, MAGIC, MAGIC, ALU.add, ALU.subtract))
                after()
                step(nc.vector.scalar_tensor_tensor(pb, q, -float(P), rank, ALU.mult, ALU.add))
                qe = flat(q).unsqueeze(2).to_broadcast([P, BE, LT])
                its = consts[:, C_IT:C_IT + LT].unsqueeze(1).to_broadcast([P, BE, LT])
                ti = tile_is[:, :, :, :].rearrange("p i e a -> p (i e) a")
                step(nc.vector.tensor_tensor(ti, its, qe, ALU.is_equal))
                after()
                tok = columns(C_TOK, b).rearrange("p i e -> p (i e)").unsqueeze(2).to_broadcast([P, BE, LT])
                step(nc.vector.tensor_tensor(ti, ti, tok, ALU.mult))
                after()
                assert n[0] == PLACES

            def b_hot(b):
                iota = consth[:, H_IOTA:H_IOTA + P].unsqueeze(1).to_broadcast([P, NT, P])
                for e in range(E):
                    if e >= 2:
                        dve.wait_ge(oh_used, b * (E - 1) + e - 1)
                    nc.vector.tensor_tensor(ohot[:, e % 2, :, :], iota, pb[:, :, e:e + 1].to_broadcast([P, NT, P]),
                                            ALU.is_equal).then_inc(oh_ready, 1)

            def b_slots(b):
                ps = full(dve, b, ("slot", 0))
                read(nc.vector.tensor_tensor(flat(slot_sum[:, :, :]), ps[:, 0:E * LT], flat(slot_sum[:, :, :]),
                                             ALU.add), ("slot", 0))

            def step_rows(f, b):
                if f is not None:
                    f_stats(f)
                if b is not None:
                    b_max(b)
                if f is not None:
                    f_wmax(f)
                if b is not None:
                    b_s(b)
                if f is not None:
                    f_norm(f)
                    f_xmax(f)
                if b is not None:
                    b_quant(b)
                if f is not None:
                    f_s(f)
                if b is not None:
                    b_dscale(b)
                if f is not None:
                    f_quant(f)
                if b is not None:
                    b_out(b)
                if f is not None:
                    f_wscale(f)
                if b is not None:
                    b_stats(b)
                    b_norm(b)
                if f is not None:
                    f_h(f)
                if b is not None:
                    b_top(b)
                if f is not None:
                    f_a(f)
                if b is not None:
                    b_place(b)
                    b_hot(b)
                    b_slots(b)

            for r in range(2 * RING):
                nc.vector.memset(cells[:, 16 + r:17 + r], 0.0).then_inc(ring_free[r], 1)
            nc.vector.memset(cells[:, 24:25], 0.0).then_inc(y_sb, 2)
            nc.vector.memset(cells[:, 25:26], 0.0).then_inc(yo_free, 1)
            nc.vector.memset(cells[:, 26:27], 0.0).then_inc(rows_st, 1)
            nc.vector.memset(slot_sum[:, :, :], 0.0).then_inc(zeroed, 1)
            nc.vector.memset(taken_n[:, :], 0.0).then_inc(zeroed, 1)
            nc.vector.memset(wrow, 0.0).then_inc(zeroed, 1)
            dve.wait_ge(zeroed, 3)
            dve.wait_ge(const_in, 16 * 5)
            dve.wait_ge(tanh_done, 1)
            rows_of_batches(dve, step_rows)

            dve.wait_ge(x1_st, 16 * B)
            dve.wait_ge(rows_st, 1 + 16 * B)
            dve.wait_ge(w_lo, 3 * E)
            taken(dve, B - 1, ("pre", 0))
            taken(dve, B - 1, ("slot", 0))
            n = [0]

            def step(ins):
                n[0] += 1
                ins.then_inc(t_step, 1)
                dve.wait_ge(t_step, n[0])

            nc.vector.tensor_copy(slots, flat(slot_sum[:, :, :])).then_inc(r_slots, 1)
            step(nc.vector.tensor_scalar(te, taken_n[:, :], 1.0 / P, (P - 1.0) / P - 127.5 / 256, ALU.mult, ALU.add))
            step(nc.vector.memset(ones8, 1.0))
            step(nc.vector.tensor_scalar(te, te, MAGIC, MAGIC, ALU.add, ALU.subtract))
            step(nc.vector.tensor_tensor_scan(incl, ones8, te, 0.0, ALU.mult, ALU.add))
            tiles1 = consts[:, C_G1:C_G1 + TCOLS]
            step(nc.vector.tensor_tensor(ended, tiles1.unsqueeze(2).to_broadcast([P, TCOLS, E]),
                                         incl.unsqueeze(1).to_broadcast([P, TCOLS, E]), ALU.is_gt))
            step(nc.vector.tensor_tensor(ended_te, ended, te.unsqueeze(1).to_broadcast([P, TCOLS, E]), ALU.mult))
            step(nc.vector.tensor_reduce(cnt, ended, AX.X, ALU.add))
            step(nc.vector.tensor_reduce(fst, ended_te, AX.X, ALU.add))
            step(nc.vector.tensor_scalar(t_expert, cnt, float(E - 1), None, ALU.min))
            step(nc.vector.tensor_scalar(t_wcol, cnt, float(D), None, ALU.add))
            step(nc.vector.scalar_tensor_tensor(tmp_t, cnt, float(LT), tiles1, ALU.mult, ALU.add))
            step(nc.vector.tensor_tensor(tmp_t, tmp_t, fst, ALU.subtract))
            nc.vector.tensor_scalar(t_list, tmp_t, -1.0, float(E * LT - 1), ALU.add, ALU.min).then_inc(r_tables, 1)
            dve.wait_ge(r_tables, 1)
            def x_to_sbuf(g, q):
                s = q % 2
                col = dve.value_load(nth(t_wcol[0:1, :], g), min_val=D, max_val=D + E)
                dve.wait_ge(xT_ps, g + 1)
                nc.vector.tensor_copy(xT[s].rearrange("p a b -> p (a b)").bitcast(i32),
                                      bank[s][:, :].bitcast(i32)).then_inc(xT_sb, 1)
                nc.vector.tensor_copy(nth(wcols, g), xg[q].bitcast(f32)[:, bass.ds(col, 1)]).then_inc(wcol_done, 1)

            def h_tile(g, s):
                dve.wait_ge(sil_ready, g + 1)
                nc.vector.scalar_tensor_tensor(hf[s], bank[2 + s][:, F:2 * F], HS / (XS * WS), sil[s],
                                               ALU.mult, ALU.mult).then_inc(hf_ready, 1)
                dve.wait_ge(hhi_ready, g + 1)
                nc.vector.tensor_tensor(hp[s][:, 1, :], hf[s], hp[s][:, 0, :], ALU.subtract).then_inc(hlo_ready, 1)

            def hT_tile(g, s):
                dve.wait_ge(hT_ps, g + 1)
                nc.vector.tensor_copy(hT[s].rearrange("p a b -> p (a b)").bitcast(i32),
                                      bank[4 + s][:, 0:F].bitcast(i32)).then_inc(hT_sb, 1)

            def tile(g, q):
                hT_tile(g, q % 2)
                if exists(g + 2):
                    x_to_sbuf(g + 2, (q + 2) % AHEAD)
                if exists(g + 1):
                    h_tile(g + 1, (q + 1) % 2)

            x_to_sbuf(0, 0)
            x_to_sbuf(1, 1)
            h_tile(0, 0)
            tiles(dve, tile)


        @block.scalar
        def _(act):
            act.preload_act_table(ACT.Silu)
            act.wait_ge(const_in, 16 * 5)
            nc.scalar.activation(gate[:, :], gate[:, :], ACT.Tanh).then_inc(tanh_done, 1)
            act.wait_ge(tanh_done, 1)

            def expert_parts(e):
                for k in range(3):
                    act.wait_ge(stage_ld[k], e * 16 + 16)
                    st = stage_w[k]
                    c = CD if k < 2 else F // P
                    if k < 2:
                        dst = w13[:, e, :, 0, k * F:(k + 1) * F] if isinstance(e, int) else \
                            w13[:, bass.ds(e, 1), :, 0, k * F:(k + 1) * F].rearrange("p e c f -> p (e c) f")
                    else:
                        dst = wdn[:, e, :, 0, :] if isinstance(e, int) else \
                            wdn[:, bass.ds(e, 1), :, 0, :].rearrange("p e c f -> p (e c) f")
                    nc.scalar.activation(dst, st.rearrange("p (c f) -> p c f", c=c), ACT.Copy, scale=WS).then_inc(w_hi, 1)
                    nc.scalar.activation(st, st, ACT.Copy, scale=WS).then_inc(wscaled, 1)

            def from_ring(b, use, dst, cols=512):
                ps = full(act, b, use)
                read(nc.scalar.activation(dst, ps[:, 0:cols], ACT.Copy), use)

            def quantized(b, use, dst):
                ps = full(act, b, use)
                read(nc.scalar.activation(dst, ps[:, :], ACT.Identity, bias=nmag), use)

            def quantize(b, buf, inv, scale_done, done):
                act.wait_ge(scale_done, b * 2 + 2)
                for j in range(4):
                    nc.scalar.activation(buf[:, j, :], buf[:, j, :], ACT.Identity, bias=mag,
                                         scale=inv[:, j:j + 1]).then_inc(done, 1)

            def b_high(b):
                act.wait_ge(rows_st, b * 16 + 1)
                for i in range(NT):
                    act.wait_ge(x2_done, b * NT + i + 1)
                    nc.scalar.activation(part(0)[:, i, :], x2[:, i, :], ACT.Copy).then_inc(hi_done, 1)

            def b_router(b):
                for i in range(NT):
                    ps = full(act, b, ("y", i))
                    if i >= 2:
                        act.wait_ge(rt_done, b * (NT - 1) + i - 1)
                    read(nc.scalar.activation(x2T[:, i % 2, :, :].rearrange("p c t -> p (c t)"), ps[:, :],
                                              ACT.Copy), ("y", i))
                ps = full(act, b, ("l", 0))
                read(nc.scalar.activation(lg.rearrange("p i e -> p (i e)"), ps[:, 0:BE], ACT.Copy, scale=1.0 / XS),
                     ("l", 0))

            def step_rows(f, b):
                if b is not None:
                    from_ring(b, ("s2", 0), s2_row, F1)
                if f is not None:
                    from_ring(f, ("s", 0), s_row)
                if b is not None:
                    for c in range(CF):
                        quantized(b, ("aq", c), aqT[:, c, :])
                    quantize(b, d_in, div, dsc_done, dq_done)
                    for c in range(CF):
                        quantized(b, ("dq", c), dqT[:, c, :])
                    ps = full(act, b, ("ds", 0))
                    read(nc.scalar.activation(dsc_row, ps[:, :], ACT.Identity, scale=gate[:, 0:1]), ("ds", 0))
                if f is not None:
                    expert_parts(f * 2)
                    for c in range(CD):
                        quantized(f, ("xq", c), xqT[:, c, :])
                    quantize(f, w_in, wiv, wsc_done, wq_done)
                    for c in range(CD):
                        quantized(f, ("wq", c), wqT[:, c, :])
                    from_ring(f, ("ws", 0), wsc_row)
                if b is not None:
                    act.wait_ge(x1_done, b * NT + NT)
                    act.dma_start(row_of(out_v, b), x_res).then_inc(x1_st, 16)
                    b_high(b)
                if f is not None:
                    for i in range(NT):
                        taken(act, f, ("h", i))
                        nc.scalar.activation(hb[:, i, 0:F1], hb[:, i, 0:F1], ACT.Silu).then_inc(silu_done, 1)
                if b is not None:
                    b_router(b)
                if f is not None:
                    expert_parts(f * 2 + 1)
                if b is not None:
                    act.wait_ge(lo_done, b * NT + NT)
                    act.wait_ge(r_w, b + 1)
                    act.dma_start(row_of(rows_v, b), row_words).then_inc(rows_st, 16)

            rows_of_batches(act, step_rows)

            def silu_high(g, s):
                act.wait_ge(gu_ready, g + 1)
                nc.scalar.activation(sil[s], bank[2 + s][:, 0:F], ACT.Silu, scale=1.0 / (XS * WS)).then_inc(sil_ready, 1)
                act.wait_ge(hf_ready, g + 1)
                nc.scalar.activation(hp[s][:, 0, :], hf[s], ACT.Copy).then_inc(hhi_ready, 1)

            def tile(g, q):
                s = q % 2
                if exists(g + 1):
                    silu_high(g + 1, 1 - s)
                act.wait_ge(y_ps, g + 1)
                if not isinstance(g, int) or g >= 1:
                    act.wait_ge(yo_free, g)
                act.wait_ge(wcol_done, g + 1)
                nc.scalar.activation(yo[s], bank[6 + s][:, :], ACT.Copy, scale=nth(wcols, g)).then_inc(y_sb, 1)

            silu_high(0, 0)
            tiles(act, tile)

        @block.gpsimd
        def _(pool):
            half, nhalf = consts[:, C_HALF:C_HALF + 4], consts[:, C_NHALF:C_NHALF + 4]
            pool.wait_ge(const_in, 16 * 5)

            def passed(c):
                return nc.gpsimd.tensor_tensor(gate_cell[:, c:c + 1], consts[:, C_E:C_E + 1], consts[:, C_E:C_E + 1], ALU.mult)

            def low_parts(e):
                pool.wait_ge(w_hi, e * 3 + 3)
                pool.wait_ge(wscaled, e * 3 + 3)
                if not isinstance(e, int):
                    passed(3)
                for k in range(3):
                    c = CD if k < 2 else F // P
                    src, lo = (w13, k * F) if k < 2 else (wdn, 0)
                    n = F if k < 2 else D
                    if isinstance(e, int):
                        hi_, lo_ = src[:, e, :, 0, lo:lo + n], src[:, e, :, 1, lo:lo + n]
                    else:
                        hi_, lo_ = (src[:, bass.ds(e, 1), :, h, lo:lo + n].rearrange("p e c f -> p (e c) f")
                                    for h in (0, 1))
                    nc.gpsimd.tensor_tensor(lo_, stage_w[k].rearrange("p (c f) -> p c f", c=c), hi_,
                                            ALU.subtract).then_inc(w_lo, 1)

            def f_rstd(b):
                pool.wait_ge(mv_done, b * NT + NT)
                nc.gpsimd.tensor_tensor(rstd, mv[:, :, 1], consts[:, C_EPS:C_EPS + NT], ALU.add).then_inc(rstd_done, 1)
                pool.wait_ge(rstd_done, b * 2 + 1)
                nc.gpsimd.tensor_tensor(rstd, rstd, nhalf, ALU.pow).then_inc(rstd_done, 1)

            def step_rows(f, b):
                if f is not None:
                    f_rstd(f)
                if b is not None:
                    pool.wait_ge(ratio2_done, b + 1)
                    nc.gpsimd.tensor_tensor(s2v, ratio2, half[:, 0:CF], ALU.pow).then_inc(sqrt2_done, 1)
                if f is not None:
                    pool.wait_ge(ratio_done, f + 1)
                    nc.gpsimd.tensor_tensor(sv, ratio, half, ALU.pow).then_inc(sqrt_done, 1)
                if b is not None:
                    taken(pool, b, ("s2", 0))
                    for j in range(D // P):
                        nc.gpsimd.tensor_tensor(d_in[:, j, :], d_in[:, j, :], s2_row, ALU.mult).then_inc(ds_done, 1)
                if f is not None:
                    taken(pool, f, ("s", 0))
                    for j in range(O1 // P):
                        nc.gpsimd.tensor_tensor(w_in[:, j, :], w_in[:, j, :], s_row, ALU.mult).then_inc(ws_done, 1)
                if b is not None:
                    pool.wait_ge(xr_ld, b * 16 + 16)
                    for i in range(NT):
                        taken(pool, b, ("o", i))
                        nc.gpsimd.tensor_tensor(x_res[:, i, :], o_tmp[:, i % 2, :], x_res[:, i, :],
                                                ALU.add).then_inc(x1_done, 1)
                    pool.wait_ge(mv2_done, b * NT + NT)
                    nc.gpsimd.tensor_tensor(rstd2, mv2[:, :, 1], consts[:, C_EPS:C_EPS + NT], ALU.add).then_inc(rstd2_done, 1)
                    pool.wait_ge(rstd2_done, b * 3 + 1)
                    nc.gpsimd.tensor_tensor(rstd2, rstd2, nhalf, ALU.pow).then_inc(rstd2_done, 1)
                    pool.wait_ge(rstd2_done, b * 3 + 2)
                    nc.gpsimd.tensor_tensor(rstd2, rstd2, xs_const, ALU.mult).then_inc(rstd2_done, 1)
                if f is not None:
                    low_parts(f * 2)
                if b is not None:
                    for i in range(NT):
                        pool.wait_ge(hi_done, b * NT + i + 1)
                        nc.gpsimd.tensor_tensor(part(1)[:, i, :], x2[:, i, :], part(0)[:, i, :],
                                                ALU.subtract).then_inc(lo_done, 1)
                    pool.wait_ge(r_diff, b + 1)
                    nc.gpsimd.tensor_tensor(ex[:, :], consts[:, C_E:C_E + NT], diff[:, :], ALU.pow).then_inc(r_exp, 1)
                if f is not None:
                    low_parts(f * 2 + 1)

            rows_of_batches(pool, step_rows)

            pool.wait_ge(r_tables, 1)
            pool.wait_ge(r_slots, 1)

            def list_column(g):
                col = pool.value_load(nth(t_list[0:1, :], g), min_val=0, max_val=E * LT - 1)
                return slots[:, bass.ds(col, 1)]

            def gather(g, q_):
                nc.gpsimd.tensor_copy(idx_g[:, q_:q_ + 1], list_column(g)).then_inc(idx_g_done, 1)
                pool.wait_ge(idx_g_done, g + 1)
                passed(1)
                pool.indirect_dma_start(xg[q_], None, rows, bass.IndirectOffsetOnAxis(idx_g[:, q_:q_ + 1], 0)
                                        ).then_inc(gathered[q_], 16)

            def tile(g, q_):
                s = q_ % 2
                if exists(g + AHEAD):
                    pool.wait_ge(xT_ps, g + 1)
                    pool.wait_ge(wcol_done, g + 1)
                    passed(0)
                    gather(g + AHEAD, q_)
                nc.gpsimd.tensor_copy(idx_s[:, s:s + 1], list_column(g)).then_inc(idx_s_done, 1)
                pool.wait_ge(idx_s_done, g + 1)
                pool.wait_ge(y_sb, g + 1 + 2)
                if isinstance(g, int) and g == 0:
                    passed(2)
                else:
                    pool.wait_ge(scattered, g * 16)
                    passed(2).then_inc(yo_free, 1)
                pool.indirect_dma_start(out_rows, bass.IndirectOffsetOnAxis(idx_s[:, s:s + 1], 0), yo[s], None,
                                        compute_op=ALU.add).then_inc(scattered, 16)

            for g in range(AHEAD):
                gather(g, g)
            tiles(pool, tile)
            for q_ in range(AHEAD):
                pool.wait_ge(gathered[q_], 16 * ((TCOLS - 1 - q_) // AHEAD + 1))
            pool.wait_ge(scattered, 16 * TILES)

        @block.tensor
        def _(pe):
            pe.wait_ge(const_in, 16 * 5)

            def spread(b, use, vec_, n):
                ps = vacant(pe, b, use)
                for c in range(n):
                    ins = nc.tensor.transpose(ps[:, c * P:(c + 1) * P], vec_[:, c:c + 1].to_broadcast([P, P]), ident)
                made(ins, use)

            def turned(b, use, src, chunks, ready=None):
                for c in range(chunks):
                    ps = vacant(pe, b, (use, c))
                    for i in range(NT):
                        if ready is not None and c == 0:
                            pe.wait_ge(ready, b * NT + i + 1)
                        ins = nc.tensor.transpose(ps[:, i * P:(i + 1) * P], src[:, i, c * P:(c + 1) * P], ident)
                    made(ins, (use, c))

            def product(b, use, lhs, rhs, chunks):
                for i in range(NT):
                    ps = vacant(pe, b, (use, i))
                    for c in range(chunks):
                        ins = nc.tensor.matmul(ps[:, :], lhs[:, c, i * P:(i + 1) * P], rhs[:, c, :],
                                               start=c == 0, stop=c == chunks - 1)
                    made(ins, (use, i))

            def b_router(b):
                for i in range(NT):
                    pe.wait_ge(x2_done, b * NT + i + 1)
                    ps = vacant(pe, b, ("y", i))
                    for c in range(CD):
                        ins = nc.tensor.transpose(ps[:, c * P:(c + 1) * P], x2[:, i, c * P:(c + 1) * P], ident)
                    made(ins, ("y", i))
                ps = vacant(pe, b, ("l", 0))
                for i in range(NT):
                    taken(pe, b, ("y", i))
                    for c in range(CD):
                        ins = nc.tensor.matmul(ps[:, i * E:(i + 1) * E], x2T[:, i % 2, c, :], router[:, c, :],
                                               start=c == 0, stop=c == CD - 1)
                    if i < NT - 1:
                        ins.then_inc(rt_done, 1)
                made(ins, ("l", 0))

            def b_place(b):
                pe.wait_ge(r_mask, b + 1)
                ps = vacant(pe, b, ("tot", 0))
                made(nc.tensor.matmul(ps[0:BE, 0:P], mask16[:, :], consth[:, H_ONE:H_ONE + P], start=True, stop=True),
                     ("tot", 0))
                taken(pe, b, ("tot", 0))
                ps = vacant(pe, b, ("pre", 0))
                nc.tensor.matmul(ps[:, BE:BE + E], tot16[:, :], consth[0:BE, H_SUM:H_SUM + E], start=True, stop=True)
                nc.tensor.matmul(ps[:, 0:BE], tot16[:, :], consth[0:BE, H_PRE:H_PRE + BE], start=True, stop=False)
                made(nc.tensor.matmul(ps[:, 0:BE], consth[:, H_TRI:H_TRI + P], mask16[:, :], start=False, stop=True),
                     ("pre", 0))
                pe.wait_ge(r_place, b * PLACES + PLACES)
                ps = vacant(pe, b, ("slot", 0))
                for e in range(E):
                    pe.wait_ge(oh_ready, b * E + e + 1)
                    for i in range(NT):
                        ins = nc.tensor.matmul(ps[:, e * LT:(e + 1) * LT], ohot[:, e % 2, i, :], tile_is[:, i, e, :],
                                               start=i == 0, stop=i == NT - 1)
                    if e < E - 1:
                        ins.then_inc(oh_used, 1)
                made(ins, ("slot", 0))

            def step_rows(f, b):
                if f is not None:
                    pe.wait_ge(w_ld, f * 16 + 16)
                    turned(f, "w", w_in, CD)
                if b is not None:
                    pe.wait_ge(d_ld, b * 16 + 16)
                    turned(b, "d", d_in, CF)
                    turned(b, "a", ab, CF, a_done)
                    pe.wait_ge(s2_done, b * 2 + 2)
                    spread(b, ("s2", 0), s2v, CF)
                    spread(b, ("r2", 0), r2v, CF)
                if f is not None:
                    turned(f, "x", xn, CD, xn_done)
                    pe.wait_ge(s_done, f * 2 + 2)
                    spread(f, ("s", 0), sv, CD)
                    spread(f, ("r", 0), rv, CD)
                if b is not None:
                    turned(b, "aq", ab, CF, aq_done)
                    turned(b, "dq", d_in, CF, dq_done)
                    spread(b, ("ds", 0), dsc, D // P)
                    for c in range(CF):
                        taken(pe, b, ("aq", c))
                        taken(pe, b, ("dq", c))
                    product(b, "o", aqT, dqT, CF)
                if f is not None:
                    turned(f, "xq", xn, CD, xq_done)
                    turned(f, "wq", w_in, CD, wq_done)
                    spread(f, ("ws", 0), wsc, O1 // P)
                    for c in range(CD):
                        taken(pe, f, ("xq", c))
                        taken(pe, f, ("wq", c))
                    product(f, "h", xqT, wqT, CD)
                if b is not None:
                    b_router(b)
                    b_place(b)

            rows_of_batches(pe, step_rows)

            pe.wait_ge(r_tables, 1)

            def turn_x(g, q):
                ps = bank[q % 2][:, :].bitcast(f16)
                pe.wait_ge(gathered[q], (g - q) * (16 // AHEAD) + 16)
                for j in range(2 * CD):
                    ins = nc.tensor.transpose(ps[:, j * P:(j + 1) * P], xg[q][:, 0:D].bitcast(f16)[:, j * P:(j + 1) * P], ident16)
                ins.then_inc(xT_ps, 1)

            def three(ps, lhs, rhs, chunks):
                for c in range(chunks):
                    nc.tensor.matmul(ps, lhs(0, c), rhs(c, 0), start=c == 0, stop=False)
                    nc.tensor.matmul(ps, lhs(0, c), rhs(c, 1), start=False, stop=False)
                for c in range(chunks):
                    ins = nc.tensor.matmul(ps, lhs(1, c), rhs(c, 0), start=False, stop=c == chunks - 1)
                return ins

            def expert_of(g):
                return pe.value_load(nth(t_expert[0:1, :], g), min_val=0, max_val=E - 1)

            def gate_up(g, s):
                e = expert_of(g)
                pe.wait_ge(xT_sb, g + 1)
                three(bank[2 + s][:, :], lambda h, c: xT[s][:, h * CD + c, :],
                      lambda c, h: w13[:, bass.ds(e, 1), c, h, :].rearrange("p e f -> p (e f)"), CD).then_inc(gu_ready, 1)

            def turn_h(g, s):
                ps = bank[4 + s][:, 0:F].bitcast(f16)
                pe.wait_ge(hhi_ready, g + 1)
                pe.wait_ge(hlo_ready, g + 1)
                for h in range(2):
                    for c in range(F // P):
                        j = h * (F // P) + c
                        ins = nc.tensor.transpose(ps[:, j * P:(j + 1) * P], hp[s][:, h, c * P:(c + 1) * P], ident16)
                ins.then_inc(hT_ps, 1)

            def down(g, s):
                e = expert_of(g)
                pe.wait_ge(hT_sb, g + 1)
                pe.wait_ge(y_sb, g + 1)
                three(bank[6 + s][:, :], lambda h, c: hT[s][:, h * (F // P) + c, :],
                      lambda c, h: wdn[:, bass.ds(e, 1), c, h, :].rearrange("p e f -> p (e f)"), F // P).then_inc(y_ps, 1)

            def tile(g, q):
                s = q % 2
                if exists(g + 1):
                    gate_up(g + 1, 1 - s)
                turn_h(g, s)
                if exists(g + 2):
                    turn_x(g + 2, (q + 2) % AHEAD)
                down(g, s)

            turn_x(0, 0)
            turn_x(1, 1)
            gate_up(0, 0)
            tiles(pe, tile)



_INS = ["x", "fside_BxS2xS2_0", "ctx_1024", "g_xattn", "g_ffn", "L0_ffn_w_router", "L0_ffn_w1", "L0_ffn_w3", "L0_ffn_w2"]


def kernel(**inputs):
    import concourse.bacc as bacc
    from concourse.bass_utils import run_bass_kernel_spmd

    nc = bacc.Bacc("TRN2", target_bir_lowering=False, num_devices=1)
    arrays, args = {}, []
    tables = dict(zip(("table_f32", "table_f16"), constant_tables()))
    for name in _INS + list(tables):
        a = np.ascontiguousarray(tables[name] if name in tables else inputs[name])
        arrays[f"in_{name}"] = a
        args.append(nc.dram_tensor(f"in_{name}", a.shape, mybir.dt.from_np(a.dtype), kind="ExternalInput").ap())
    args.append(nc.dram_tensor("out_0", (B, T, D), mybir.dt.float32, kind="ExternalOutput").ap())
    build(nc, *args)
    r = run_bass_kernel_spmd(nc, [arrays], core_ids=[0])
    return r.results[0]["out_0"]
```

```python
from contextlib import ExitStack

import numpy as np

import concourse.bass as bass
from concourse import mybir

P = 128
B, T, D, F1 = 4, 512, 512, 256
E, F = 8, 256
O1 = 2 * F1
NT = T // P
CD, CF = D // P, F1 // P
NTOK = B * T
CH = NTOK // P
TILES = (2 * NTOK + E * (P - 1)) // P
AHEAD = 4
TCOLS = TILES + 2
assert (TILES - 3) % AHEAD == 0
EW = 16
LT = NTOK // P
ROW = D + EW
EPS = 1e-6
QMAX = 127.0
LN_EPS = 1e-5
MAGIC = 1.5 * 2.0 ** 23
XS, WS, HS = 2.0 ** 8, 2.0 ** 8, 2.0 ** 6

C_ID, C_REV, C_G1 = 0, P, 2 * P
C_MAG = C_G1 + TCOLS
C_NMAG, C_HALF, C_NHALF, C_E, C_IE, C_END = (C_MAG + n for n in (1, 2, 6, 10, 14, 14 + E))
H_ID, H_TRI, H_ONE, H_PRE, H_SUM, H_IOTA, H_TOK, H_IT, H_END = 0, 128, 256, 384, 416, 424, 552, 680, 696
BE = NT * E


def constant_tables():
    p = np.arange(P)
    f = np.zeros((P, C_END), np.float32)
    token = np.repeat(np.arange(CH), E)[None, :] * P + p[:, None]
    f[:, C_ID:C_ID + P] = np.eye(P)
    f[:, C_REV:C_REV + P] = token - (NTOK - 1)
    f[:, C_G1:C_G1 + TCOLS] = np.arange(TCOLS)[None, :] + 1
    f[:, C_MAG], f[:, C_NMAG] = MAGIC, -MAGIC
    f[:, C_HALF:C_HALF + 4], f[:, C_NHALF:C_NHALF + 4] = 0.5, -0.5
    f[:, C_E:C_E + 4] = np.e
    f[:, C_IE:C_IE + E] = np.arange(E)
    h = np.zeros((P, H_END), np.float16)
    h[:, H_ID:H_ID + P] = np.eye(P)
    h[:, H_TRI:H_TRI + P] = p[:, None] < p[None, :]
    h[:, H_ONE:H_ONE + P] = 1.0
    ie = np.arange(BE)
    same = (ie % E)[:, None] == (ie % E)[None, :]
    h[:BE, H_PRE:H_PRE + BE] = same & ((ie // E)[:, None] < (ie // E)[None, :])
    h[:BE, H_SUM:H_SUM + E] = (ie % E)[:, None] == np.arange(E)[None, :]
    h[:, H_TOK:H_TOK + P] = token
    h[:, H_IT:H_IT + LT] = np.arange(LT)
    h[:, H_IOTA:H_IOTA + P] = p[None, :]
    return f, h


RING = 4
FRONT = ([("w", c) for c in range(CD)] + [("x", c) for c in range(CD)] + [("s", 0), ("r", 0)]
         + [("xq", c) for c in range(CD)] + [("wq", c) for c in range(CD)] + [("ws", 0)] + [("h", i) for i in range(NT)])
BACK = ([("d", c) for c in range(CF)] + [("a", c) for c in range(CF)] + [("s2", 0), ("r2", 0)]
        + [("aq", c) for c in range(CF)] + [("dq", c) for c in range(CF)] + [("ds", 0)] + [("o", i) for i in range(NT)]
        + [("y", i) for i in range(NT)] + [("l", 0), ("slot", 0), ("tot", 0), ("pre", 0)])
PLACE = {}
for base, uses in ((0, FRONT), (RING, BACK)):
    for n, u in enumerate(uses):
        PLACE[u] = (base + n % RING, n // RING + 1, len(range(n % RING, len(uses), RING)))


def build(nc, x, guw, dww, gx, gf, wr, w1, w3, w2, cf, ch, out):
    f32, f16, bf16 = mybir.dt.float32, mybir.dt.float16, mybir.dt.bfloat16
    i32, u32 = mybir.dt.int32, mybir.dt.uint32
    ALU, ACT, AX = mybir.AluOpType, mybir.ActivationFunctionType, mybir.AxisListType
    ctx = ExitStack()
    with ctx:
        def sb(name, shape, dt=f32):
            return ctx.enter_context(nc.sbuf_tensor(name, shape, dt))

        def sem(name):
            return ctx.enter_context(nc.semaphore(name))

        x_v = x.rearrange("b (i p) d -> b p i d", p=P)
        w_v = guw.rearrange("b (i p) d -> b p i d", p=P)
        d_v = dww.rearrange("b (i p) d -> b p i d", p=P)
        out_rows = out.rearrange("b t d -> (b t) d")
        out_v = out.rearrange("b (i p) d -> b p i d", p=P)
        rows = nc.dram_tensor("rows", [NTOK, ROW], i32).ap()
        rows_v = rows.rearrange("(b i p) n -> b p i n", p=P, i=NT)
        w1_v = w1.rearrange("e (c p) f -> e p c f", p=P)
        w3_v = w3.rearrange("e (c p) f -> e p c f", p=P)
        w2_v = w2.rearrange("e (c p) d -> e p c d", p=P)

        consts = sb("consts", [P, C_END])
        consth = sb("consth", [P, H_END], f16)
        w13 = sb("w13", [P, E, CD, 2, 2 * F], f16)
        wdn = sb("wdn", [P, E, F // P, 2, D], f16)
        router = sb("router", [P, CD, E])
        gate = sb("gate", [P, 2])
        gate_cell = sb("gate_cell", [P, 8])
        cells = sb("cells", [P, 32])
        small = sb("small", [P, 192])
        slot_sum = sb("slot_sum", [P, E, LT])
        taken_n = sb("taken_n", [P, E])
        arena_words = 26620
        arena = sb("arena", [P, arena_words])
        at = [0]

        def carve(shape, dt=f32):
            n = int(np.prod(shape))
            size = n if dt in (f32, i32, u32) else n // 2
            v = arena[:, at[0]:at[0] + size]
            at[0] += size
            assert at[0] <= arena_words, at[0]
            if dt is not f32:
                v = v.bitcast(dt)
            if len(shape) == 2:
                v = v.rearrange("p (a b) -> p a b", a=shape[0])
            if len(shape) == 3:
                v = v.rearrange("p (a b c) -> p a b c", a=shape[0], b=shape[1])
            return v

        x_in = carve([NT, D])
        w_in = carve([O1 // P, D])
        xn = carve([NT, D])
        hb = carve([NT, O1])
        xqT = carve([CD, T], bf16)
        wqT = carve([CD, O1], bf16)
        s_row, wsc_row = carve([D]), carve([O1])
        ab = carve([NT, F1])
        d_in = carve([D // P, F1])
        aqT = carve([CF, T], bf16)
        dqT = carve([CF, D], bf16)
        s2_row, dsc_row = carve([F1]), carve([D])
        x_res = carve([NT, D])
        x2 = carve([NT, D])
        x2T = xn.rearrange("p i (c t) -> p i c t", c=CD)
        row_words = carve([NT, ROW], i32)
        ohot = carve([E, NT, P], f16)
        stage_w = [carve([1024]) for _ in range(3)]

        def part(h):
            return row_words[:, :, h * (D // 2):(h + 1) * (D // 2)].bitcast(f16)

        wrow = row_words[:, :, D:ROW].bitcast(f32)
        at[0] = 0
        xg = [carve([ROW], i32) for _ in range(AHEAD)]
        xT = [carve([2 * CD, P], f16) for _ in range(2)]
        sil = [carve([F]) for _ in range(2)]
        hf = [carve([F]) for _ in range(2)]
        hp = [carve([2, F], f16) for _ in range(2)]
        hT = [carve([2 * F // P, P], f16) for _ in range(2)]
        yo = [carve([D]) for _ in range(2)]
        slots = carve([E * LT], u32)
        idx_g, idx_s = carve([AHEAD], u32), carve([2], u32)
        wcols = carve([TCOLS])
        t_expert, t_wcol, t_list = carve([TCOLS], i32), carve([TCOLS], i32), carve([TCOLS], i32)
        te, incl, ones8 = carve([E]), carve([E]), carve([E])
        ended, ended_te = carve([TCOLS, E]), carve([TCOLS, E])
        cnt, fst, tmp_t = carve([TCOLS]), carve([TCOLS]), carve([TCOLS])

        ident = consts[:, C_ID:C_ID + P]
        ident16 = consth[:, H_ID:H_ID + P]
        mag, nmag = consts[:, C_MAG:C_MAG + 1], consts[:, C_NMAG:C_NMAG + 1]
        used = [0]

        def vec(n):
            used[0] += n
            return small[:, used[0] - n:used[0]]

        bns = vec(24).rearrange("p (i s) -> p i s", i=NT)
        mv = vec(8).rearrange("p (i s) -> p i s", i=NT)
        rstd, wmax, xmax, winv, ratio = vec(NT), vec(CD), vec(CD), vec(CD), vec(CD)
        sv, rv = vec(CD), vec(CD)
        xrm, xsc, xiv = vec(NT), vec(NT), vec(NT)
        wrm, wsc, wiv = vec(4), vec(4), vec(4)
        dmax, amax, dinv, ratio2, s2v, r2v = vec(CF), vec(CF), vec(CF), vec(CF), vec(CF), vec(CF)
        arm, asc, aiv = vec(NT), vec(NT), vec(NT)
        drm, dsc, div = vec(4), vec(4), vec(4)
        bns2 = vec(24).rearrange("p (i s) -> p i s", i=NT)
        mv2 = vec(8).rearrange("p (i s) -> p i s", i=NT)
        rstd2 = vec(NT)
        var1, nmean1, bias1, var2, nmean2, bias2 = (vec(NT) for _ in range(6))
        route_f = sb("route_f", [P, 11, NT, E])
        lg, mx, idf, first1, first2, mask, idle, rank, q, pb, tmp = (route_f[:, k] for k in range(11))
        mi = sb("mi", [P, NT, E], u32)
        diff, ex, den, p1, p2 = (sb(n, [P, NT]) for n in ("diff", "ex", "den", "p1", "p2"))
        mask16 = sb("mask16", [P, BE], f16)
        tile16, slot16 = sb("tile16", [P, NT, E], f16), sb("slot16", [P, NT, E], f16)
        tot16 = sb("tot16", [BE, P], f16)
        tile_is = sb("tile_is", [P, NT, E, LT], f16)

        bank = [ctx.enter_context(nc.psum_tensor(f"bank{n}", [P, 512], f32)) for n in range(8)]

        ring_full = [sem(f"ring_full{r}") for r in range(2 * RING)]
        ring_free = [sem(f"ring_free{r}") for r in range(2 * RING)]
        const_in, x_ld, w_ld, d_ld, xr_ld = sem("const_in"), sem("x_ld"), sem("w_ld"), sem("d_ld"), sem("xr_ld")
        stage_ld = [sem(f"stage_ld{k}") for k in range(3)]
        bn_done, mv_done, rstd_done, xn_done = sem("bn_done"), sem("mv_done"), sem("rstd_done"), sem("xn_done")
        winv_done, ratio_done, sqrt_done, s_done = sem("winv_done"), sem("ratio_done"), sem("sqrt_done"), sem("s_done")
        ws_done, wrm_done, wsc_done, wq_done = sem("ws_done"), sem("wrm_done"), sem("wsc_done"), sem("wq_done")
        xs_done, xsc_done, xq_done = sem("xs_done"), sem("xsc_done"), sem("xq_done")
        silu_done, a_done = sem("silu_done"), sem("a_done")
        dinv_done, ratio2_done, sqrt2_done, s2_done = sem("dinv_done"), sem("ratio2_done"), sem("sqrt2_done"), sem("s2_done")
        as_done, asc_done, aq_done = sem("as_done"), sem("asc_done"), sem("aq_done")
        ds_done, drm_done, dsc_done, dq_done = sem("ds_done"), sem("drm_done"), sem("dsc_done"), sem("dq_done")
        x1_done, x1_st = sem("x1_done"), sem("x1_st")
        bn2_done, mv2_done, rstd2_done, x2_done = sem("bn2_done"), sem("mv2_done"), sem("rstd2_done"), sem("x2_done")
        hi_done, lo_done, rows_st = sem("hi_done"), sem("lo_done"), sem("rows_st")
        tanh_done, wscaled, w_hi, w_lo = sem("tanh_done"), sem("wscaled"), sem("w_hi"), sem("w_lo")
        r_step, r_mask, r_diff, r_exp, r_w = sem("r_step"), sem("r_mask"), sem("r_diff"), sem("r_exp"), sem("r_w")
        oh_ready, slots_last = sem("oh_ready"), sem("slots_last")
        r_tables, r_slots = sem("r_tables"), sem("r_slots")
        yo_free = sem("yo_free")
        idx_g_done, idx_s_done = sem("idx_g_done"), sem("idx_s_done")
        gathered = [sem(f"gathered{q_}") for q_ in range(AHEAD)]
        xT_ps, xT_sb, wcol_done = sem("xT_ps"), sem("xT_sb"), sem("wcol_done")
        gu_ready, sil_ready, hf_ready = sem("gu_ready"), sem("sil_ready"), sem("hf_ready")
        hhi_ready, hlo_ready, hT_ps, hT_sb = sem("hhi_ready"), sem("hlo_ready"), sem("hT_ps"), sem("hT_sb")
        y_ps, y_sb, scattered = sem("y_ps"), sem("y_sb"), sem("scattered")

        def full(eng, b, use):
            r, n, per = PLACE[use]
            eng.wait_ge(ring_full[r], b * per + n)
            return bank[r]

        def vacant(eng, b, use):
            r, n, per = PLACE[use]
            eng.wait_ge(ring_free[r], b * per + n)
            return bank[r]

        def taken(eng, b, use):
            r, n, per = PLACE[use]
            eng.wait_ge(ring_free[r], b * per + n + 1)

        def made(ins, use):
            ins.then_inc(ring_full[PLACE[use][0]], 1)

        def read(ins, use):
            ins.then_inc(ring_free[PLACE[use][0]], 1)

        def rows_of_batches(eng, step):
            step(0, None)
            with eng.Fori(1, B - 1) as b:
                step(b, b - 1)
            step(B - 1, B - 2)
            step(None, B - 1)

        def first(f):
            return isinstance(f, int) and f == 0

        def w_share(f):
            return range(O1 // P if first(f) else 1)

        def row_after(f):
            return f is not None and not (isinstance(f, int) and f == B - 1)

        def tiles(eng, body):
            body(0, 0)
            with eng.Fori(0, (TILES - 3) // AHEAD) as turn:
                for k in range(1, AHEAD + 1):
                    body(turn * AHEAD + k, k % AHEAD)
            body(TILES - 2, (TILES - 2) % AHEAD)
            body(TILES - 1, (TILES - 1) % AHEAD)

        def exists(g):
            return not isinstance(g, int) or g < TILES

        def nth(v, g):
            return v[:, g:g + 1] if isinstance(g, int) else v[:, bass.ds(g, 1)]

        def columns(table, lo, b):
            v = table[:, lo:lo + P].rearrange("p (b n) -> p b n", b=B)
            v = v[:, b, :] if isinstance(b, int) else v[:, bass.ds(b, 1), :].rearrange("p b n -> p (b n)")
            return v.rearrange("p (i e) -> p i e", i=NT)

        o_tmp = ab.rearrange("p i f -> p (i f)").rearrange("p (k d) -> p k d", k=2)
        zeroed, r_place, t_step = sem("zeroed"), sem("r_place"), sem("t_step")
        WARM = 20
        tok_done = sem("tok_done")
        PLACES = 12

        block = ctx.enter_context(nc.Block())


        @block.sync
        def _(sp):
            sp.dma_start(x_in, x_v[0]).then_inc(x_ld, 16)
            sp.dma_start(consts[:, :], cf).then_inc(const_in, 16)
            sp.dma_start(consth[:, :], ch).then_inc(const_in, 16)
            sp.dma_start(gate[:, 0:1], gx.rearrange("(o a) -> o a", o=1).to_broadcast([P, 1])).then_inc(const_in, 16)
            sp.dma_start(gate[:, 1:2], gf.rearrange("(o a) -> o a", o=1).to_broadcast([P, 1])).then_inc(const_in, 16)
            sp.dma_start(router[:, :, :], wr.rearrange("(c p) e -> p c e", p=P)).then_inc(const_in, 16)
            sp.dma_start(w_in, w_v[0]).then_inc(w_ld, 16)

            def load_expert(e):
                for k, v in enumerate((w1_v, w3_v, w2_v)):
                    if e >= 1:
                        sp.wait_ge(w_lo, e * 3 - 2 + k)
                    a = CD if k < 2 else F // P
                    sp.dma_start(stage_w[k].rearrange("p (c f) -> p c f", c=a), v[e]).then_inc(stage_ld[k], 16)

            load_expert(0)
            def store_x1(b):
                sp.wait_ge(x1_done, b * NT + NT)
                sp.dma_start(out_v[b], x_res).then_inc(x1_st, 16)

            def store_rows(b):
                sp.wait_ge(lo_done, b * NT + NT)
                sp.wait_ge(r_w, b + 1)
                sp.dma_start(rows_v[b], row_words).then_inc(rows_st, 16)

            for b in range(B):
                if b + 1 < B:
                    sp.wait_ge(xn_done, NT * (b + 1))
                    sp.dma_start(x_in, x_v[b + 1]).then_inc(x_ld, 16)
                if b == 0:
                    load_expert(1)
                if b >= 1:
                    full(sp, b - 1, ("dq", CF - 1))
                sp.dma_start(d_in, d_v[b]).then_inc(d_ld, 16)
                if b + 1 < B:
                    full(sp, b, ("wq", CD - 1))
                    sp.dma_start(w_in, w_v[b + 1]).then_inc(w_ld, 16)
                if b >= 1:
                    store_x1(b - 1)
                load_expert(b + 2)
                if b >= 1:
                    sp.wait_ge(x1_st, 16 * b)
                    sp.wait_ge(x2_done, NT * b)
                sp.dma_start(x_res, x_v[b]).then_inc(xr_ld, 16)
                if b >= 1:
                    store_rows(b - 1)
            load_expert(E - 2)
            store_x1(B - 1)
            load_expert(E - 1)
            store_rows(B - 1)

        @block.vector
        def _(dve):
            def absmax(b, use, dst):
                ps = full(dve, b, use)
                read(nc.vector.tensor_reduce(dst, ps[:, :], AX.X, ALU.max, apply_absolute_value=True), use)

            def row_scale(b, rm, sc, iv, rm_done, nrm, done):
                dve.wait_ge(rm_done, nrm)
                nc.vector.tensor_scalar(sc, rm, EPS, 1.0 / QMAX, ALU.max, ALU.mult).then_inc(done, 1)
                dve.wait_ge(done, b * 2 + 1)
                nc.vector.reciprocal(iv, sc).then_inc(done, 1)

            def inverse_max(b, m, inv, done, last_use):
                for u in last_use:
                    taken(dve, b, u)
                nc.vector.tensor_scalar(inv, m, EPS, None, ALU.max).then_inc(done, 1)
                dve.wait_ge(done, b * 2 + 1)
                nc.vector.reciprocal(inv, inv).then_inc(done, 1)

            def s_and_inverse(b, v, inv, root_done, done):
                dve.wait_ge(root_done, b + 1)
                nc.vector.tensor_scalar(v, v, EPS, None, ALU.max).then_inc(done, 1)
                dve.wait_ge(done, b * 2 + 1)
                nc.vector.reciprocal(inv, v).then_inc(done, 1)

            def statistics(b, src, st, ag, vs, nm, scale, st_done, ag_done, cell, per_tile=None):
                for i in range(NT):
                    if per_tile is not None:
                        dve.wait_ge(per_tile, b * NT + i + 1)
                        nc.vector.memset(cells[:, cell + 1 + i:cell + 2 + i], 0.0)
                    nc.vector.bn_stats(st[:, i, :], src[:, i, :]).then_inc(st_done, 1)
                dve.wait_ge(st_done, b * NT + NT)
                nc.vector.memset(cells[:, cell:cell + 1], 0.0)
                for i in range(NT):
                    nc.vector.bn_aggr(ag[:, i, :], st[:, i, :]).then_inc(ag_done, 1)
                dve.wait_ge(ag_done, b * (NT + 2) + NT)
                nc.vector.tensor_scalar(vs, ag[:, :, 1], LN_EPS, 1.0 / scale ** 2, ALU.add, ALU.mult).then_inc(ag_done, 1)
                nc.vector.tensor_scalar(nm, ag[:, :, 0], -1.0, None, ALU.mult).then_inc(ag_done, 1)

            def scaled(b, buf, width, use, rm, sc, iv, done, sc_done):
                ps = full(dve, b, use)
                for i in range(NT):
                    ins = nc.vector.tensor_tensor(buf[:, i, :], buf[:, i, :], ps[:, 0:width], ALU.mult)
                    if i < NT - 1:
                        ins.then_inc(done, 1)
                    else:
                        read(ins, use)
                dve.wait_ge(done, b * NT + NT - 1)
                taken(dve, b, use)
                nc.vector.tensor_reduce(rm, buf, AX.X, ALU.max, apply_absolute_value=True).then_inc(done, 1)
                row_scale(b, rm, sc, iv, done, b * NT + NT, sc_done)

            def f_stats(b):
                dve.wait_ge(x_ld, b * 16 + 16)
                statistics(b, x_in, bns, mv, var1, nmean1, 1.0, bn_done, mv_done, 0)

            def f_wmax(b):
                for c in range(CD):
                    absmax(b, ("w", c), wmax[:, c:c + 1])
                inverse_max(b, wmax, winv, winv_done, [("w", c) for c in range(CD)])

            def f_xmax(b):
                for c in range(CD):
                    absmax(b, ("x", c), xmax[:, c:c + 1])
                for c in range(CD):
                    taken(dve, b, ("x", c))
                dve.wait_ge(winv_done, b * 2 + 2)
                nc.vector.scalar_tensor_tensor(ratio, xmax, EPS, winv, ALU.max, ALU.mult).then_inc(ratio_done, 1)

            def f_s(b):
                s_and_inverse(b, sv, rv, sqrt_done, s_done)

            def f_scale(b):
                scaled(b, xn, D, ("r", 0), xrm, xsc, xiv, xs_done, xsc_done)

            def f_wscale(b):
                for j in range(O1 // P):
                    dve.wait_ge(ws_done, b * 4 + j + 1)
                    nc.vector.tensor_reduce(wrm[:, j:j + 1], w_in[:, j, :], AX.X, ALU.max,
                                            apply_absolute_value=True).then_inc(wrm_done, 1)
                row_scale(b, wrm, wsc, wiv, wrm_done, b * 4 + 4, wsc_done)

            def f_h(b):
                taken(dve, b, ("ws", 0))
                for i in range(NT):
                    ps = full(dve, b, ("h", i))
                    read(nc.vector.scalar_tensor_tensor(hb[:, i, :], ps[:, :], xsc[:, i:i + 1], wsc_row,
                                                        ALU.mult, ALU.mult), ("h", i))

            def b_max(b):
                for c in range(CF):
                    absmax(b, ("d", c), dmax[:, c:c + 1])
                inverse_max(b, dmax, dinv, dinv_done, [("d", c) for c in range(CF)])
                for c in range(CF):
                    absmax(b, ("a", c), amax[:, c:c + 1])
                for c in range(CF):
                    taken(dve, b, ("a", c))
                dve.wait_ge(dinv_done, b * 2 + 2)
                nc.vector.scalar_tensor_tensor(ratio2, amax, EPS, dinv, ALU.max, ALU.mult).then_inc(ratio2_done, 1)

            def b_s(b):
                s_and_inverse(b, s2v, r2v, sqrt2_done, s2_done)

            def b_scale(b):
                scaled(b, ab, F1, ("r2", 0), arm, asc, aiv, as_done, asc_done)

            def quantize(b, buf, iv, sc_done, done, which=range(NT)):
                dve.wait_ge(sc_done, b * 2 + 2)
                for i in which:
                    nc.vector.tensor_scalar(buf[:, i, :], buf[:, i, :], iv[:, i:i + 1], MAGIC,
                                            ALU.mult, ALU.add).then_inc(done, 1)

            def b_dscale(b):
                dve.wait_ge(ds_done, b * 4 + 4)
                nc.vector.tensor_reduce(drm, d_in, AX.X, ALU.max, apply_absolute_value=True).then_inc(drm_done, 1)
                row_scale(b, drm, dsc, div, drm_done, b + 1, dsc_done)

            def b_hot(experts):
                iota = consth[:, H_IOTA:H_IOTA + P].unsqueeze(1).to_broadcast([P, NT, P])
                for e in experts:
                    nc.vector.tensor_tensor(ohot[:, e, :, :], iota, slot16[:, :, e:e + 1].to_broadcast([P, NT, P]),
                                            ALU.is_equal).then_inc(oh_ready, 1)

            def b_out(b):
                taken(dve, b, ("ds", 0))
                for i in range(NT):
                    if i >= 2:
                        b_hot(range(i - 2, i - 1))
                        dve.wait_ge(x1_done, b * NT + i - 1)
                    ps = full(dve, b, ("o", i))
                    read(nc.vector.scalar_tensor_tensor(o_tmp[:, i % 2, :], ps[:, :], asc[:, i:i + 1], dsc_row,
                                                        ALU.mult, ALU.mult), ("o", i))

            def b_stats(b):
                statistics(b, x_res, bns2, mv2, var2, nmean2, XS, bn2_done, mv2_done, 5, per_tile=x1_done)

            def over_experts(v):
                return v.unsqueeze(2).to_broadcast([P, NT, E])

            def over_tiles(v):
                return v.unsqueeze(1).to_broadcast([P, NT, E])

            def flat(v):
                return v.rearrange("p a b -> p (a b)")

            STEPS = 13

            def b_top(b):
                n = [0]

                def step(ins):
                    n[0] += 1
                    ins.then_inc(r_step, 1)

                def after():
                    dve.wait_ge(r_step, b * STEPS + n[0])

                taken(dve, b, ("l", 0))
                nc.vector.memset(cells[:, 10:11], 0.0)
                for i in range(NT):
                    step(nc.vector.max(mx[:, i, :], lg[:, i, :]))
                after()
                nc.vector.memset(cells[:, 11:12], 0.0)
                for i in range(NT):
                    step(nc.vector.max_index(mi[:, i, :], mx[:, i, :], lg[:, i, :]))
                nc.vector.tensor_tensor(diff[:, :], mx[:, :, 1], mx[:, :, 0], ALU.subtract).then_inc(r_diff, 1)
                after()
                step(nc.vector.tensor_copy(idf, mi[:, :, :]))
                after()
                experts = over_tiles(consts[:, C_IE:C_IE + E])
                step(nc.vector.tensor_tensor(first1, experts, over_experts(idf[:, :, 0]), ALU.is_equal))
                step(nc.vector.tensor_tensor(first2, experts, over_experts(idf[:, :, 1]), ALU.is_equal))
                after()
                nc.vector.tensor_tensor(mask16[:, :].rearrange("p (a b) -> p a b", a=NT), first1, first2,
                                        ALU.add).then_inc(r_mask, 1)
                step(nc.vector.tensor_tensor(mask, first1, first2, ALU.add))
                after()
                step(nc.vector.scalar_tensor_tensor(idle, mask, 1.0, columns(consts, C_REV, b), ALU.subtract, ALU.mult))
                assert n[0] == STEPS

            def b_place(b):
                n = [0]

                def step(ins):
                    n[0] += 1
                    ins.then_inc(r_place, 1)

                def after():
                    dve.wait_ge(r_place, b * PLACES + n[0])

                dve.wait_ge(r_step, b * STEPS + STEPS)
                dve.wait_ge(r_exp, b + 1)
                step(nc.vector.tensor_scalar(den[:, :], ex[:, :], 1.0, None, ALU.add))
                after()
                step(nc.vector.reciprocal(p1[:, :], den[:, :]))
                ps = full(dve, b, ("tot", 0))
                read(nc.vector.tensor_copy(tot16[:, :], ps[0:BE, 0:P]), ("tot", 0))
                after()
                step(nc.vector.tensor_tensor(p2[:, :], ex[:, :], p1[:, :], ALU.mult))
                step(nc.vector.tensor_tensor(tmp, first1, over_experts(p1[:, :]), ALU.mult))
                after()
                step(nc.vector.tensor_tensor(pb, first2, over_experts(p2[:, :]), ALU.mult))
                after()
                step(nc.vector.tensor_tensor(tmp, tmp, pb, ALU.add))
                dve.wait_ge(rows_st, b * 16 + 1)
                after()
                nc.vector.tensor_scalar(wrow[:, :, 0:E], tmp, gate[:, 1:2], 1.0 / (HS * WS),
                                        ALU.mult, ALU.mult).then_inc(r_w, 1)
                ps = full(dve, b, ("pre", 0))
                step(nc.vector.tensor_tensor(rank, ps[:, 0:BE].rearrange("p (a b) -> p a b", a=NT), idle, ALU.add))
                after()
                step(nc.vector.tensor_tensor(rank, rank, over_tiles(taken_n[:, :]), ALU.add))
                after()
                read(nc.vector.tensor_tensor(taken_n[:, :], ps[:, BE:BE + E], taken_n[:, :], ALU.add), ("pre", 0))
                step(nc.vector.tensor_scalar(q, rank, 1.0 / P, -127.5 / 256, ALU.mult, ALU.add))
                after()
                step(nc.vector.tensor_scalar(tile16[:, :, :], q, MAGIC, MAGIC, ALU.add, ALU.subtract))
                after()
                step(nc.vector.scalar_tensor_tensor(slot16[:, :, :], tile16[:, :, :], -float(P), rank, ALU.mult, ALU.add))
                qe = flat(tile16[:, :, :]).unsqueeze(2).to_broadcast([P, BE, LT])
                its = consth[:, H_IT:H_IT + LT].unsqueeze(1).to_broadcast([P, BE, LT])
                ti = tile_is[:, :, :, :].rearrange("p i e a -> p (i e) a")
                step(nc.vector.tensor_tensor(ti, its, qe, ALU.is_equal))
                after()
                assert n[0] == PLACES

            def b_norm(b):
                dve.wait_ge(rstd2_done, b * 2 + 1)
                for i in range(NT):
                    nc.vector.tensor_scalar(x2[:, i, :], x_res[:, i, :], mv2[:, i, 0:1], rstd2[:, i:i + 1],
                                            ALU.subtract, ALU.mult).then_inc(x2_done, 1)

            def b_slots(b):
                ps = full(dve, b, ("slot", 0))
                read(nc.vector.tensor_tensor(flat(slot_sum[:, :, :]), ps[:, 0:E * LT], flat(slot_sum[:, :, :]),
                                             ALU.add), ("slot", 0))

            def step_rows(f, b):
                if first(f):
                    f_stats(0)
                if b is not None:
                    b_max(b)
                if f is not None:
                    f_wmax(f)
                if b is not None:
                    b_s(b)
                if f is not None:
                    f_xmax(f)
                if b is not None:
                    b_scale(b)
                if f is not None:
                    f_s(f)
                if b is not None:
                    quantize(b, ab, aiv, asc_done, aq_done)
                if b is not None:
                    b_dscale(b)
                    if f is None:
                        quantize(b, d_in, div, dsc_done, dq_done)
                if f is not None:
                    f_scale(f)
                    f_wscale(f)
                    quantize(f, w_in, wiv, wsc_done, wq_done, w_share(f))
                if b is not None:
                    b_out(b)
                    b_stats(b)
                    b_hot(range(2, 4))
                    if f is None:
                        b_norm(b)
                    b_hot(range(4, 6))
                if f is not None:
                    f_h(f)
                if b is not None:
                    b_hot(range(6, E))
                if row_after(f):
                    f_stats(f + 1)
                if b is not None:
                    b_top(b)
                    b_slots(b)
                    b_place(b)

            for r in range(2 * RING):
                nc.vector.memset(cells[:, 16 + r:17 + r], 0.0).then_inc(ring_free[r], 1)
            nc.vector.memset(cells[:, 24:25], 0.0).then_inc(y_sb, 2)
            nc.vector.memset(cells[:, 25:26], 0.0).then_inc(yo_free, 1)
            nc.vector.memset(cells[:, 26:27], 0.0).then_inc(rows_st, 1)
            nc.vector.memset(cells[:, 27:28], 0.0).then_inc(tok_done, 1)
            nc.vector.memset(slot_sum[:, :, :], 0.0).then_inc(zeroed, 1)
            nc.vector.memset(taken_n[:, :], 0.0).then_inc(zeroed, 1)
            nc.vector.memset(wrow, 0.0).then_inc(zeroed, 1)
            nc.vector.memset(slot16[:, :, :], 0.0).then_inc(zeroed, 1)
            nc.vector.memset(tile_is[:, :, :, :], 0.0).then_inc(zeroed, 1)
            dve.wait_ge(zeroed, 5)
            dve.wait_ge(const_in, 16 * 5)
            dve.wait_ge(tanh_done, 1)
            rows_of_batches(dve, step_rows)
            b_hot(range(E))

            taken(dve, B - 1, ("pre", 0))
            n = [0]

            def step(ins):
                n[0] += 1
                ins.then_inc(t_step, 1)
                dve.wait_ge(t_step, n[0])

            step(nc.vector.tensor_scalar(te, taken_n[:, :], 1.0 / P, (P - 1.0) / P - 127.5 / 256, ALU.mult, ALU.add))
            step(nc.vector.memset(ones8, 1.0))
            step(nc.vector.tensor_scalar(te, te, MAGIC, MAGIC, ALU.add, ALU.subtract))
            step(nc.vector.tensor_tensor_scan(incl, ones8, te, 0.0, ALU.mult, ALU.add))
            tiles1 = consts[:, C_G1:C_G1 + TCOLS]
            step(nc.vector.tensor_tensor(ended, tiles1.unsqueeze(2).to_broadcast([P, TCOLS, E]),
                                         incl.unsqueeze(1).to_broadcast([P, TCOLS, E]), ALU.is_gt))
            step(nc.vector.tensor_tensor(ended_te, ended, te.unsqueeze(1).to_broadcast([P, TCOLS, E]), ALU.mult))
            step(nc.vector.tensor_reduce(cnt, ended, AX.X, ALU.add))
            step(nc.vector.tensor_reduce(fst, ended_te, AX.X, ALU.add))
            step(nc.vector.tensor_scalar(t_expert, cnt, float(E - 1), None, ALU.min))
            step(nc.vector.tensor_scalar(t_wcol, cnt, float(D), None, ALU.add))
            step(nc.vector.scalar_tensor_tensor(tmp_t, cnt, float(LT), tiles1, ALU.mult, ALU.add))
            step(nc.vector.tensor_tensor(tmp_t, tmp_t, fst, ALU.subtract))
            nc.vector.tensor_scalar(t_list, tmp_t, -1.0, float(E * LT - 1), ALU.add, ALU.min).then_inc(r_tables, 1)
            dve.wait_ge(slots_last, 1)
            taken(dve, B - 1, ("slot", 0))
            nc.vector.tensor_tensor(slots, bank[0][:, 0:E * LT], flat(slot_sum[:, :, :]), ALU.add).then_inc(r_slots, 1)
            dve.wait_ge(r_tables, 1)

            def x_to_sbuf(g, q):
                s = q % 2
                col = dve.value_load(nth(t_wcol[0:1, :], g), min_val=D, max_val=D + E)
                dve.wait_ge(xT_ps, g + 1)
                nc.vector.tensor_copy(xT[s].rearrange("p a b -> p (a b)").bitcast(i32),
                                      bank[s][:, :].bitcast(i32)).then_inc(xT_sb, 1)
                nc.vector.tensor_copy(nth(wcols, g), xg[q].bitcast(f32)[:, bass.ds(col, 1)]).then_inc(wcol_done, 1)

            def h_tile(g, s):
                dve.wait_ge(sil_ready, g + 1)
                nc.vector.scalar_tensor_tensor(hf[s], bank[2 + s][:, F:2 * F], HS / (XS * WS), sil[s],
                                               ALU.mult, ALU.mult).then_inc(hf_ready, 1)
                dve.wait_ge(hhi_ready, g + 1)
                nc.vector.tensor_tensor(hp[s][:, 1, :], hf[s], hp[s][:, 0, :], ALU.subtract).then_inc(hlo_ready, 1)

            def hT_tile(g, s):
                dve.wait_ge(hT_ps, g + 1)
                nc.vector.tensor_copy(hT[s].rearrange("p a b -> p (a b)").bitcast(i32),
                                      bank[4 + s][:, 0:F].bitcast(i32)).then_inc(hT_sb, 1)

            def tile(g, q):
                hT_tile(g, q % 2)
                if exists(g + 2):
                    x_to_sbuf(g + 2, (q + 2) % AHEAD)
                if exists(g + 1):
                    h_tile(g + 1, (q + 1) % 2)

            x_to_sbuf(0, 0)
            x_to_sbuf(1, 1)
            h_tile(0, 0)
            tiles(dve, tile)


        @block.scalar
        def _(act):
            act.preload_act_table(ACT.Silu)
            act.wait_ge(const_in, 16 * 5)
            nc.scalar.activation(gate[:, :], gate[:, :], ACT.Tanh).then_inc(tanh_done, 1)
            act.wait_ge(tanh_done, 1)

            def expert_parts(e, which=range(3)):
                for k in which:
                    act.wait_ge(stage_ld[k], e * 16 + 16)
                    st = stage_w[k]
                    c = CD if k < 2 else F // P
                    if k < 2:
                        dst = w13[:, e, :, 0, k * F:(k + 1) * F] if isinstance(e, int) else \
                            w13[:, bass.ds(e, 1), :, 0, k * F:(k + 1) * F].rearrange("p e c f -> p (e c) f")
                    else:
                        dst = wdn[:, e, :, 0, :] if isinstance(e, int) else \
                            wdn[:, bass.ds(e, 1), :, 0, :].rearrange("p e c f -> p (e c) f")
                    nc.scalar.activation(dst, st.rearrange("p (c f) -> p c f", c=c), ACT.Copy, scale=WS).then_inc(w_hi, 1)
                    nc.scalar.activation(st, st, ACT.Copy, scale=WS).then_inc(wscaled, 1)

            def from_ring(b, use, dst, cols=512):
                ps = full(act, b, use)
                read(nc.scalar.activation(dst, ps[:, 0:cols], ACT.Copy), use)

            def quantized(b, use, dst):
                ps = full(act, b, use)
                read(nc.scalar.activation(dst, ps[:, :], ACT.Identity, bias=nmag), use)

            def quantize(b, buf, inv, scale_done, done, which=range(NT)):
                act.wait_ge(scale_done, b * 2 + 2)
                for j in which:
                    nc.scalar.activation(buf[:, j, :], buf[:, j, :], ACT.Identity, bias=mag,
                                         scale=inv[:, j:j + 1]).then_inc(done, 1)

            def normalize(b, src, dst, scale, bias, ready, done):
                act.wait_ge(ready, b * 2 + 2)
                for i in range(NT):
                    nc.scalar.activation(dst[:, i, :], src[:, i, :], ACT.Identity, bias=bias[:, i:i + 1],
                                         scale=scale[:, i:i + 1]).then_inc(done, 1)

            def b_high(b):
                act.wait_ge(rows_st, b * 16 + 1)
                for i in range(NT):
                    act.wait_ge(x2_done, b * NT + i + 1)
                    nc.scalar.activation(part(0)[:, i, :], x2[:, i, :], ACT.Copy).then_inc(hi_done, 1)

            def b_turned(b):
                for i in range(NT):
                    ps = full(act, b, ("y", i))
                    read(nc.scalar.activation(x2T[:, i, :, :].rearrange("p c t -> p (c t)"), ps[:, :],
                                              ACT.Copy), ("y", i))

            def b_logits(b):
                ps = full(act, b, ("l", 0))
                read(nc.scalar.activation(lg.rearrange("p i e -> p (i e)"), ps[:, 0:BE], ACT.Copy, scale=1.0 / XS),
                     ("l", 0))

            def step_rows(f, b):
                if f is not None:
                    normalize(f, x_in, xn, rstd, bias1, rstd_done, xn_done)
                    expert_parts(0 if first(f) else f + 1)
                else:
                    expert_parts(E - 3)
                if b is not None:
                    from_ring(b, ("s2", 0), s2_row, F1)
                if f is not None:
                    from_ring(f, ("s", 0), s_row)
                if first(f):
                    expert_parts(1, range(0, 2))
                if b is not None:
                    for c in range(CF):
                        quantized(b, ("aq", c), aqT[:, c, :])
                    if f is not None:
                        quantize(b, d_in, div, dsc_done, dq_done)
                    for c in range(CF):
                        quantized(b, ("dq", c), dqT[:, c, :])
                    ps = full(act, b, ("ds", 0))
                    read(nc.scalar.activation(dsc_row, ps[:, :], ACT.Identity, scale=gate[:, 0:1]), ("ds", 0))
                if f is None:
                    expert_parts(E - 2)
                if f is not None:
                    quantize(f, xn, xiv, xsc_done, xq_done)
                    quantize(f, w_in, wiv, wsc_done, wq_done, range(len(w_share(f)), O1 // P))
                    for c in range(CD):
                        quantized(f, ("xq", c), xqT[:, c, :])
                    for c in range(CD):
                        quantized(f, ("wq", c), wqT[:, c, :])
                    from_ring(f, ("ws", 0), wsc_row)
                if first(f):
                    expert_parts(1, range(2, 3))
                if b is not None:
                    if f is not None:
                        normalize(b, x_res, x2, rstd2, bias2, rstd2_done, x2_done)
                    b_turned(b)
                if f is not None:
                    for i in range(NT):
                        taken(act, f, ("h", i))
                        nc.scalar.activation(hb[:, i, 0:F1], hb[:, i, 0:F1], ACT.Silu).then_inc(silu_done, 1)
                if b is not None:
                    if f is None:
                        b_high(b)
                        b_logits(b)
                    else:
                        b_logits(b)
                        b_high(b)
                if f is None:
                    expert_parts(E - 1)

            rows_of_batches(act, step_rows)

            def silu_high(g, s):
                act.wait_ge(gu_ready, g + 1)
                nc.scalar.activation(sil[s], bank[2 + s][:, 0:F], ACT.Silu, scale=1.0 / (XS * WS)).then_inc(sil_ready, 1)
                act.wait_ge(hf_ready, g + 1)
                nc.scalar.activation(hp[s][:, 0, :], hf[s], ACT.Copy).then_inc(hhi_ready, 1)

            def tile(g, q):
                s = q % 2
                if exists(g + 1):
                    silu_high(g + 1, 1 - s)
                act.wait_ge(y_ps, g + 1)
                if not isinstance(g, int) or g >= 1:
                    act.wait_ge(yo_free, g)
                act.wait_ge(wcol_done, g + 1)
                nc.scalar.activation(yo[s], bank[6 + s][:, :], ACT.Copy, scale=nth(wcols, g)).then_inc(y_sb, 1)

            silu_high(0, 0)
            tiles(act, tile)

        @block.gpsimd
        def _(pool):
            half, nhalf = consts[:, C_HALF:C_HALF + 4], consts[:, C_NHALF:C_NHALF + 4]
            pool.wait_ge(const_in, 16 * 5)

            def passed(c):
                one = consts[:, C_E:C_E + 1]
                return nc.gpsimd.tensor_tensor(gate_cell[:, c:c + 1], one, one, ALU.mult)

            def low_parts(e, which=range(3)):
                for k in which:
                    pool.wait_ge(w_hi, e * 3 + k + 1)
                    pool.wait_ge(wscaled, e * 3 + k + 1)
                    c = CD if k < 2 else F // P
                    src, lo = (w13, k * F) if k < 2 else (wdn, 0)
                    n = F if k < 2 else D
                    if isinstance(e, int):
                        hi_, lo_ = src[:, e, :, 0, lo:lo + n], src[:, e, :, 1, lo:lo + n]
                    else:
                        passed(4 + k)
                        hi_, lo_ = (src[:, bass.ds(e, 1), :, h, lo:lo + n].rearrange("p e c f -> p (e c) f")
                                    for h in (0, 1))
                    nc.gpsimd.tensor_tensor(lo_, stage_w[k].rearrange("p (c f) -> p c f", c=c), hi_,
                                            ALU.subtract).then_inc(w_lo, 1)

            def low_rows(b, which):
                for i in which:
                    pool.wait_ge(hi_done, b * NT + i + 1)
                    nc.gpsimd.tensor_tensor(part(1)[:, i, :], x2[:, i, :], part(0)[:, i, :],
                                            ALU.subtract).then_inc(lo_done, 1)

            def f_a(b):
                for i in range(NT):
                    pool.wait_ge(silu_done, b * NT + i + 1)
                    taken(pool, b, ("h", i))
                    nc.gpsimd.tensor_tensor(ab[:, i, :], hb[:, i, 0:F1], hb[:, i, F1:O1], ALU.mult).then_inc(a_done, 1)

            def inverse_root(b, vs, nm, root, bias, mean_done, done):
                pool.wait_ge(mean_done, (b + 1) * (NT + 2))
                nc.gpsimd.tensor_tensor(root, vs, nhalf, ALU.pow).then_inc(done, 1)
                pool.wait_ge(done, b * 2 + 1)
                nc.gpsimd.tensor_tensor(bias, nm, root, ALU.mult).then_inc(done, 1)

            def step_rows(f, b):
                if first(f):
                    inverse_root(0, var1, nmean1, rstd, bias1, mv_done, rstd_done)
                    low_parts(0, range(0, 1))
                if b is not None:
                    pool.wait_ge(ratio2_done, b + 1)
                    nc.gpsimd.tensor_tensor(s2v, ratio2, half[:, 0:CF], ALU.pow).then_inc(sqrt2_done, 1)
                if f is None:
                    low_parts(E - 3, range(0, 1))
                if f is not None:
                    pool.wait_ge(ratio_done, f + 1)
                    nc.gpsimd.tensor_tensor(sv, ratio, half, ALU.pow).then_inc(sqrt_done, 1)
                    if first(f):
                        low_parts(0, range(1, 2))
                if b is not None:
                    taken(pool, b, ("s2", 0))
                    for j in range(D // P):
                        nc.gpsimd.tensor_tensor(d_in[:, j, :], d_in[:, j, :], s2_row, ALU.mult).then_inc(ds_done, 1)
                if f is None:
                    low_parts(E - 3, range(1, 3))
                if f is not None:
                    taken(pool, f, ("s", 0))
                    for j in range(O1 // P):
                        nc.gpsimd.tensor_tensor(w_in[:, j, :], w_in[:, j, :], s_row, ALU.mult).then_inc(ws_done, 1)
                    if first(f):
                        low_parts(0, range(2, 3))
                if b is not None:
                    pool.wait_ge(xr_ld, b * 16 + 16)
                    for i in range(NT):
                        taken(pool, b, ("o", i))
                        nc.gpsimd.tensor_tensor(x_res[:, i, :], o_tmp[:, i % 2, :], x_res[:, i, :],
                                                ALU.add).then_inc(x1_done, 1)
                    inverse_root(b, var2, nmean2, rstd2, bias2, mv2_done, rstd2_done)
                low_parts(E - 2 if f is None else 1 if first(f) else f + 1)
                if f is not None:
                    f_a(f)
                if b is not None:
                    early = range(0, 2 if f is None else 0)
                    low_rows(b, early)
                    pool.wait_ge(r_diff, b + 1)
                    nc.gpsimd.tensor_tensor(ex[:, :], consts[:, C_E:C_E + NT], diff[:, :], ALU.pow).then_inc(r_exp, 1)
                if row_after(f):
                    inverse_root(f + 1, var1, nmean1, rstd, bias1, mv_done, rstd_done)
                if b is not None:
                    low_rows(b, range(len(early), NT))
                    pool.wait_ge(r_place, b * PLACES + PLACES)
                    ti = tile_is[:, :, :, :].rearrange("p i e a -> p (i e) a")
                    tok = columns(consth, H_TOK, b).rearrange("p i e -> p (i e)").unsqueeze(2).to_broadcast([P, BE, LT])
                    passed(7)
                    nc.gpsimd.tensor_tensor(ti, ti, tok, ALU.mult).then_inc(tok_done, 1)
                if f is None:
                    low_parts(E - 1)

            rows_of_batches(pool, step_rows)

            pool.wait_ge(r_tables, 1)
            pool.wait_ge(r_slots, 1)
            pool.wait_ge(rows_st, 1 + 16 * B)
            pool.wait_ge(x1_st, 16 * B)

            def list_column(g):
                col = pool.value_load(nth(t_list[0:1, :], g), min_val=0, max_val=E * LT - 1)
                return slots[:, bass.ds(col, 1)]

            def gather(g, q_):
                nc.gpsimd.tensor_copy(idx_g[:, q_:q_ + 1], list_column(g)).then_inc(idx_g_done, 1)
                pool.wait_ge(idx_g_done, g + 1)
                passed(1)
                pool.indirect_dma_start(xg[q_], None, rows, bass.IndirectOffsetOnAxis(idx_g[:, q_:q_ + 1], 0)
                                        ).then_inc(gathered[q_], 16)

            def tile(g, q_):
                s = q_ % 2
                if exists(g + AHEAD):
                    pool.wait_ge(xT_ps, g + 1)
                    pool.wait_ge(wcol_done, g + 1)
                    passed(0)
                    gather(g + AHEAD, q_)
                nc.gpsimd.tensor_copy(idx_s[:, s:s + 1], list_column(g)).then_inc(idx_s_done, 1)
                pool.wait_ge(idx_s_done, g + 1)
                pool.wait_ge(y_sb, g + 1 + 2)
                if isinstance(g, int) and g == 0:
                    passed(2)
                else:
                    pool.wait_ge(scattered, g * 16)
                    passed(2).then_inc(yo_free, 1)
                pool.indirect_dma_start(out_rows, bass.IndirectOffsetOnAxis(idx_s[:, s:s + 1], 0), yo[s], None,
                                        compute_op=ALU.add).then_inc(scattered, 16)

            for g in range(AHEAD):
                gather(g, g)
            tiles(pool, tile)
            for q_ in range(AHEAD):
                pool.wait_ge(gathered[q_], 16 * ((TCOLS - 1 - q_) // AHEAD + 1))
            pool.wait_ge(scattered, 16 * TILES)

        @block.tensor
        def _(pe):
            pe.wait_ge(const_in, 16 * 5)

            def spread(b, use, vec_, n):
                ps = vacant(pe, b, use)
                for c in range(n):
                    ins = nc.tensor.transpose(ps[:, c * P:(c + 1) * P], vec_[:, c:c + 1].to_broadcast([P, P]), ident)
                made(ins, use)

            def turned(b, use, src, chunks, ready=None):
                for c in range(chunks):
                    ps = vacant(pe, b, (use, c))
                    for i in range(NT):
                        if ready is not None and c == 0:
                            pe.wait_ge(ready, b * NT + i + 1)
                        ins = nc.tensor.transpose(ps[:, i * P:(i + 1) * P], src[:, i, c * P:(c + 1) * P], ident)
                    made(ins, (use, c))

            def product(b, use, lhs, rhs, chunks):
                for i in range(NT):
                    ps = vacant(pe, b, (use, i))
                    for c in range(chunks):
                        ins = nc.tensor.matmul(ps[:, :], lhs[:, c, i * P:(i + 1) * P], rhs[:, c, :],
                                               start=c == 0, stop=c == chunks - 1)
                    made(ins, (use, i))

            def b_router(b):
                for i in range(NT):
                    pe.wait_ge(x2_done, b * NT + i + 1)
                    ps = vacant(pe, b, ("y", i))
                    for c in range(CD):
                        ins = nc.tensor.transpose(ps[:, c * P:(c + 1) * P], x2[:, i, c * P:(c + 1) * P], ident)
                    made(ins, ("y", i))
                ps = vacant(pe, b, ("l", 0))
                for i in range(NT):
                    taken(pe, b, ("y", i))
                    for c in range(CD):
                        ins = nc.tensor.matmul(ps[:, i * E:(i + 1) * E], x2T[:, i, c, :], router[:, c, :],
                                               start=c == 0, stop=c == CD - 1)
                made(ins, ("l", 0))

            def b_place(b):
                pe.wait_ge(r_mask, b + 1)
                ps = vacant(pe, b, ("tot", 0))
                made(nc.tensor.matmul(ps[0:BE, 0:P], mask16[:, :], consth[:, H_ONE:H_ONE + P], start=True, stop=True),
                     ("tot", 0))
                taken(pe, b, ("tot", 0))
                ps = vacant(pe, b, ("pre", 0))
                nc.tensor.matmul(ps[:, BE:BE + E], tot16[:, :], consth[0:BE, H_SUM:H_SUM + E], start=True, stop=True)
                nc.tensor.matmul(ps[:, 0:BE], tot16[:, :], consth[0:BE, H_PRE:H_PRE + BE], start=True, stop=False)
                made(nc.tensor.matmul(ps[:, 0:BE], consth[:, H_TRI:H_TRI + P], mask16[:, :], start=False, stop=True),
                     ("pre", 0))
            def slot_products(ps):
                for e in range(E):
                    for i in range(NT):
                        ins = nc.tensor.matmul(ps[:, e * LT:(e + 1) * LT], ohot[:, e, i, :], tile_is[:, i, e, :],
                                               start=i == 0, stop=i == NT - 1)
                return ins

            def b_slots(b):
                pe.wait_ge(oh_ready, b * E + E)
                pe.wait_ge(tok_done, b + 1)
                ps = vacant(pe, b, ("slot", 0))
                made(slot_products(ps), ("slot", 0))

            def step_rows(f, b):
                if b is not None:
                    pe.wait_ge(d_ld, b * 16 + 16)
                    turned(b, "d", d_in, CF)
                    turned(b, "a", ab, CF, a_done)
                if f is not None:
                    pe.wait_ge(w_ld, f * 16 + 16)
                    turned(f, "w", w_in, CD)
                    turned(f, "x", xn, CD, xn_done)
                if b is not None:
                    pe.wait_ge(s2_done, b * 2 + 2)
                    spread(b, ("s2", 0), s2v, CF)
                    spread(b, ("r2", 0), r2v, CF)
                if f is not None:
                    pe.wait_ge(s_done, f * 2 + 2)
                    spread(f, ("s", 0), sv, CD)
                    spread(f, ("r", 0), rv, CD)
                if b is not None:
                    turned(b, "aq", ab, CF, aq_done)
                    turned(b, "dq", d_in, CF, dq_done)
                    spread(b, ("ds", 0), dsc, D // P)
                    for c in range(CF):
                        taken(pe, b, ("aq", c))
                        taken(pe, b, ("dq", c))
                    product(b, "o", aqT, dqT, CF)
                if f is not None:
                    turned(f, "xq", xn, CD, xq_done)
                    pe.wait_ge(wq_done, f * (O1 // P) + O1 // P)
                    turned(f, "wq", w_in, CD)
                    spread(f, ("ws", 0), wsc, O1 // P)
                    for c in range(CD):
                        taken(pe, f, ("xq", c))
                        taken(pe, f, ("wq", c))
                    product(f, "h", xqT, wqT, CD)
                if b is not None:
                    b_router(b)
                    b_slots(b)
                    b_place(b)

            rows_of_batches(pe, step_rows)
            pe.wait_ge(oh_ready, B * E + E)
            pe.wait_ge(tok_done, B + 1)
            slot_products(bank[0]).then_inc(slots_last, 1)

            with pe.Fori(0, WARM):
                for _ in range(4):
                    nc.tensor.transpose(bank[4][:, 0:P // 2].bitcast(f16), ident16, ident16)

            pe.wait_ge(r_tables, 1)
            pe.wait_ge(w_lo, 3 * E)

            def turn_x(g, q):
                ps = bank[q % 2][:, :].bitcast(f16)
                pe.wait_ge(gathered[q], (g - q) * (16 // AHEAD) + 16)
                for j in range(2 * CD):
                    ins = nc.tensor.transpose(ps[:, j * P:(j + 1) * P], xg[q][:, 0:D].bitcast(f16)[:, j * P:(j + 1) * P], ident16)
                ins.then_inc(xT_ps, 1)

            def high_products(ps, lhs, rhs, chunks):
                for c in range(chunks):
                    nc.tensor.matmul(ps, lhs(0, c), rhs(c, 0), start=c == 0, stop=False)
                    nc.tensor.matmul(ps, lhs(0, c), rhs(c, 1), start=False, stop=False)

            def low_products(ps, lhs, rhs, chunks):
                for c in range(chunks):
                    ins = nc.tensor.matmul(ps, lhs(1, c), rhs(c, 0), start=False, stop=c == chunks - 1)
                return ins

            def expert_of(g):
                return pe.value_load(nth(t_expert[0:1, :], g), min_val=0, max_val=E - 1)

            def gate_up(g, s, between=None):
                e = expert_of(g)
                operands = (bank[2 + s][:, :], lambda h, c: xT[s][:, h * CD + c, :],
                            lambda c, h: w13[:, bass.ds(e, 1), c, h, :].rearrange("p e f -> p (e f)"), CD)
                pe.wait_ge(xT_sb, g + 1)
                high_products(*operands)
                if between:
                    between()
                low_products(*operands).then_inc(gu_ready, 1)

            def turn_h(g, s):
                ps = bank[4 + s][:, 0:F].bitcast(f16)
                pe.wait_ge(hhi_ready, g + 1)
                pe.wait_ge(hlo_ready, g + 1)
                for h in range(2):
                    for c in range(F // P):
                        j = h * (F // P) + c
                        ins = nc.tensor.transpose(ps[:, j * P:(j + 1) * P], hp[s][:, h, c * P:(c + 1) * P], ident16)
                ins.then_inc(hT_ps, 1)

            def down(g, s):
                e = expert_of(g)
                pe.wait_ge(hT_sb, g + 1)
                pe.wait_ge(y_sb, g + 1)
                operands = (bank[6 + s][:, :], lambda h, c: hT[s][:, h * (F // P) + c, :],
                            lambda c, h: wdn[:, bass.ds(e, 1), c, h, :].rearrange("p e f -> p (e f)"), F // P)
                high_products(*operands)
                low_products(*operands).then_inc(y_ps, 1)

            def tile(g, q):
                s = q % 2
                if exists(g + 1):
                    gate_up(g + 1, 1 - s, between=lambda: turn_h(g, s))
                else:
                    turn_h(g, s)
                if exists(g + 2):
                    turn_x(g + 2, (q + 2) % AHEAD)
                down(g, s)

            turn_x(0, 0)
            turn_x(1, 1)
            gate_up(0, 0)
            tiles(pe, tile)



_INS = ["x", "fside_BxS2xS2_0", "ctx_1024", "g_xattn", "g_ffn", "L0_ffn_w_router", "L0_ffn_w1", "L0_ffn_w3", "L0_ffn_w2"]


def kernel(**inputs):
    import concourse.bacc as bacc
    from concourse.bass_utils import run_bass_kernel_spmd

    nc = bacc.Bacc("TRN2", target_bir_lowering=False, num_devices=1)
    arrays, args = {}, []
    tables = dict(zip(("table_f32", "table_f16"), constant_tables()))
    for name in _INS + list(tables):
        a = np.ascontiguousarray(tables[name] if name in tables else inputs[name])
        arrays[f"in_{name}"] = a
        args.append(nc.dram_tensor(f"in_{name}", a.shape, mybir.dt.from_np(a.dtype), kind="ExternalInput").ap())
    args.append(nc.dram_tensor("out_0", (B, T, D), mybir.dt.float32, kind="ExternalOutput").ap())
    build(nc, *args)
    r = run_bass_kernel_spmd(nc, [arrays], core_ids=[0])
    return r.results[0]["out_0"]
```
